# Optimizing a Trainium2 kernel written in Bass

```python
import numpy as np
import jax
import jax.numpy as jnp

def _softmax(x, axis=-1):
    return jax.nn.softmax(x, axis=axis)

def _gelu(x):
    return jax.nn.gelu(x, approximate=True)

def _silu(x):
    return jax.nn.silu(x)

def _sigmoid(x):
    return jax.nn.sigmoid(x)

def _layernorm(x, axis=-1, eps=1e-05):
    m = jnp.mean(x, axis=axis, keepdims=True)
    v = jnp.var(x, axis=axis, keepdims=True)
    return (x - m) / jnp.sqrt(v + eps)

def _scatter_add(tgt, idx, src, axis=0):
    return tgt.at[idx].add(src)

def _segment_sum(src, seg, n):
    return jax.ops.segment_sum(src, seg, n)
kernel_name = 'mk_prb_d1_jaxref_r4_9cd21a'

def setup_inputs(seed: int=0):
    np.random.seed(seed)
    _w = jnp.asarray

    def _L0_attn_setup():
        import jax, jax.numpy as jnp
        import numpy as np
        D_MODEL = 256
        NUM_HEADS = 16
        D_K = D_MODEL // NUM_HEADS
        MAX_SEQ_LEN = 1024
        THETA = 10000.0

        def _rope_tables(seq_len):
            pos = jnp.arange(seq_len, dtype=jnp.float32)
            pair = jnp.arange(D_K // 2, dtype=jnp.float32)
            rates = THETA ** (-(2.0 * pair) / D_K)
            angles = pos[:, None] * rates[None, :]
            return (jnp.cos(angles), jnp.sin(angles))

        def _apply_rope(x, cos, sin):
            x_even = x[..., 0::2]
            x_odd = x[..., 1::2]
            r_even = x_even * cos - x_odd * sin
            r_odd = x_even * sin + x_odd * cos
            out = jnp.stack([r_even, r_odd], axis=-1)
            return out.reshape(x.shape)
        key = jax.random.key(seed)
        ks = jax.random.split(key, 5)
        x = jax.random.normal(ks[0], (1, 1024, D_MODEL), dtype=jnp.float32)
        Wq = jax.random.truncated_normal(ks[1], -2.0, 2.0, (D_MODEL, D_MODEL), dtype=jnp.float32) * D_MODEL ** (-0.5)
        Wk = jax.random.truncated_normal(ks[2], -2.0, 2.0, (D_MODEL, D_MODEL), dtype=jnp.float32) * D_MODEL ** (-0.5)
        Wv = jax.random.truncated_normal(ks[3], -2.0, 2.0, (D_MODEL, D_MODEL), dtype=jnp.float32) * D_MODEL ** (-0.5)
        Wo = jax.random.truncated_normal(ks[4], -2.0, 2.0, (D_MODEL, D_MODEL), dtype=jnp.float32) * D_MODEL ** (-0.5)
        return {'x': x, 'Wq': Wq, 'Wk': Wk, 'Wv': Wv, 'Wo': Wo}
    _L0_attn_in = _L0_attn_setup()

    def _L0_ffn_setup():
        import jax, jax.numpy as jnp
        import numpy as np
        B, S, D = (4, 512, 256)
        P = 9
        DM = D // 4
        EPS = 1e-05

        def _mix(x, mix_kernel):
            xp = jnp.pad(x, ((0, 0), (1, 1), (0, 0)))
            return mix_kernel[0] * xp[:, :-2] + mix_kernel[1] * xp[:, 1:-1] + mix_kernel[2] * xp[:, 2:]

        def _layernorm(h, gamma, beta):
            mu = jnp.mean(h, axis=-1, keepdims=True)
            var = jnp.var(h, axis=-1, keepdims=True)
            return (h - mu) * jax.lax.rsqrt(var + EPS) * gamma + beta
        key = jax.random.key(seed)
        ks = jax.random.split(key, 12)
        sc_in = 1.0 / np.sqrt(D)
        sc_mid = 1.0 / np.sqrt(DM)
        return {'x': jax.random.normal(ks[0], (B, S, D), dtype=jnp.float32), 'mix_kernel': jax.random.normal(ks[1], (3, D), dtype=jnp.float32) * 0.5, 'W1': jax.random.normal(ks[2], (P, D, DM), dtype=jnp.float32) * sc_in, 'b1': jnp.zeros((P, DM), dtype=jnp.float32), 'W2': jax.random.normal(ks[3], (P, DM, D), dtype=jnp.float32) * sc_mid, 'b2': jnp.zeros((P, D), dtype=jnp.float32), 'Wo1': jax.random.normal(ks[4], (D, DM), dtype=jnp.float32) * sc_in, 'bo1': jnp.zeros((DM,), dtype=jnp.float32), 'Wo2': jax.random.normal(ks[5], (DM, P), dtype=jnp.float32) * sc_mid, 'bo2': jnp.zeros((P,), dtype=jnp.float32), 'gamma': jnp.ones((D,), dtype=jnp.float32), 'beta': jnp.zeros((D,), dtype=jnp.float32)}
    _L0_ffn_in = _L0_ffn_setup()
    _d = {'L0_attn_x': _L0_attn_in['x'], 'L0_attn_Wq': _L0_attn_in['Wq'], 'L0_attn_Wk': _L0_attn_in['Wk'], 'L0_attn_Wv': _L0_attn_in['Wv'], 'L0_attn_Wo': _L0_attn_in['Wo'], 'L0_ffn_mix_kernel': _L0_ffn_in['mix_kernel'], 'L0_ffn_W1': _L0_ffn_in['W1'], 'L0_ffn_b1': _L0_ffn_in['b1'], 'L0_ffn_W2': _L0_ffn_in['W2'], 'L0_ffn_b2': _L0_ffn_in['b2'], 'L0_ffn_Wo1': _L0_ffn_in['Wo1'], 'L0_ffn_bo1': _L0_ffn_in['bo1'], 'L0_ffn_Wo2': _L0_ffn_in['Wo2'], 'L0_ffn_bo2': _L0_ffn_in['bo2'], 'L0_ffn_gamma': _L0_ffn_in['gamma'], 'L0_ffn_beta': _L0_ffn_in['beta']}
    _x0 = _d['L0_attn_x']
    _d['L0_attn_x'] = jax.random.normal(jax.random.fold_in(jax.random.key(seed), 1), (4, 1024, 256), dtype=_x0.dtype)
    del _x0
    return _d

def reference(L0_attn_x, L0_attn_Wq, L0_attn_Wk, L0_attn_Wv, L0_attn_Wo, L0_ffn_mix_kernel, L0_ffn_W1, L0_ffn_b1, L0_ffn_W2, L0_ffn_b2, L0_ffn_Wo1, L0_ffn_bo1, L0_ffn_Wo2, L0_ffn_bo2, L0_ffn_gamma, L0_ffn_beta):

    def _L0_attn_ref(x, Wq, Wk, Wv, Wo):
        import jax, jax.numpy as jnp
        import numpy as np
        D_MODEL = 256
        NUM_HEADS = 16
        D_K = D_MODEL // NUM_HEADS
        MAX_SEQ_LEN = 1024
        THETA = 10000.0

        def _rope_tables(seq_len):
            pos = jnp.arange(seq_len, dtype=jnp.float32)
            pair = jnp.arange(D_K // 2, dtype=jnp.float32)
            rates = THETA ** (-(2.0 * pair) / D_K)
            angles = pos[:, None] * rates[None, :]
            return (jnp.cos(angles), jnp.sin(angles))

        def _apply_rope(x, cos, sin):
            x_even = x[..., 0::2]
            x_odd = x[..., 1::2]
            r_even = x_even * cos - x_odd * sin
            r_odd = x_even * sin + x_odd * cos
            out = jnp.stack([r_even, r_odd], axis=-1)
            return out.reshape(x.shape)
        b, s, _ = x.shape

        def split_heads(t):
            return t.reshape(b, s, NUM_HEADS, D_K).transpose(0, 2, 1, 3)
        q = split_heads(x @ Wq.T)
        k = split_heads(x @ Wk.T)
        v = split_heads(x @ Wv.T)
        cos, sin = _rope_tables(s)
        q = _apply_rope(q, cos, sin)
        k = _apply_rope(k, cos, sin)
        scores = jnp.einsum('bhqd,bhkd->bhqk', q, k) / jnp.sqrt(jnp.float32(D_K))
        causal = jnp.tril(jnp.ones((s, s), dtype=bool))
        scores = jnp.where(causal, scores, jnp.float32(-1000000000.0))
        probs = jax.nn.softmax(scores, axis=-1)
        attn = jnp.einsum('bhqk,bhkd->bhqd', probs, v)
        attn = attn.transpose(0, 2, 1, 3).reshape(b, s, D_MODEL)
        return attn @ Wo.T

    def _L0_ffn_ref(x, mix_kernel, W1, b1, W2, b2, Wo1, bo1, Wo2, bo2, gamma, beta):
        import jax, jax.numpy as jnp
        import numpy as np
        B, S, D = (4, 512, 256)
        P = 9
        DM = D // 4
        EPS = 1e-05

        def _mix(x, mix_kernel):
            xp = jnp.pad(x, ((0, 0), (1, 1), (0, 0)))
            return mix_kernel[0] * xp[:, :-2] + mix_kernel[1] * xp[:, 1:-1] + mix_kernel[2] * xp[:, 2:]

        def _layernorm(h, gamma, beta):
            mu = jnp.mean(h, axis=-1, keepdims=True)
            var = jnp.var(h, axis=-1, keepdims=True)
            return (h - mu) * jax.lax.rsqrt(var + EPS) * gamma + beta
        x_mixed = _mix(x, mix_kernel)
        h = jnp.einsum('bsd,pdm->bspm', x_mixed, W1) + b1
        stacked_paths = jnp.einsum('bspm,pmd->bspd', h, W2) + b2
        scores = jnp.tanh(x_mixed @ Wo1 + bo1) @ Wo2 + bo2
        idx = jnp.argmax(scores, axis=-1)
        weights = jax.nn.one_hot(idx, P, dtype=stacked_paths.dtype)
        collapsed = jnp.einsum('bspd,bsp->bsd', stacked_paths, weights)
        return _layernorm(x + collapsed, gamma, beta)
    x = L0_attn_x
    xn = _layernorm(x, axis=-1)
    x = x + _L0_attn_ref(xn, L0_attn_Wq, L0_attn_Wk, L0_attn_Wv, L0_attn_Wo) + _L0_ffn_ref(xn, L0_ffn_mix_kernel, L0_ffn_W1, L0_ffn_b1, L0_ffn_W2, L0_ffn_b2, L0_ffn_Wo1, L0_ffn_bo1, L0_ffn_Wo2, L0_ffn_bo2, L0_ffn_gamma, L0_ffn_beta)
    return x

_drawn_inputs = setup_inputs


def setup_inputs(seed=0):
    import zlib

    import numpy as np

    out = dict(_drawn_inputs(seed))
    spreads = {'L0_ffn_b1': (0.0, 0.1),
     'L0_ffn_b2': (0.0, 0.1),
     'L0_ffn_bo1': (0.0, 0.1),
     'L0_ffn_bo2': (0.0, 0.1),
     'L0_ffn_gamma': (1.0, 0.2),
     'L0_ffn_beta': (0.0, 0.1)}
    factors = {}
    for name, (base, spread) in spreads.items():
        noise = np.random.default_rng([zlib.crc32(name.encode()), seed]).standard_normal(out[name].shape)
        drawn = base * np.exp(spread * noise) if base else spread * noise
        out[name] = jnp.asarray(drawn.astype(out[name].dtype))
    for name, factor in factors.items():
        out[name] = (out[name] * factor).astype(out[name].dtype)
    return out
```

```python
from contextlib import ExitStack

import numpy as np

import concourse.bass as bass
from concourse import mybir

ALU = mybir.AluOpType
ACT = mybir.ActivationFunctionType
AX = mybir.AxisListType
BF16 = mybir.dt.bfloat16
F32 = mybir.dt.float32

B, S, D = 4, 1024, 256
H = 16
DK = D // H
P = 128
NT = S // P
NC = D // P
PATHS = 9
DM = D // 4
MID = PATHS * DM
NJ = (MID + P - 1) // P
LAST = DM + PATHS
PARTS = 6 * DK
SHIFT = 2
VW = 32
GH = 4
NG = H // GH
RING = 8
SLOT = 1024
EPS = 1e-5
THETA = 10000.0
NEG = -1e30

STEPS = NT // 2 + 1


def step_blocks(i):
    out = [(i, 0, S - P * i)]
    if i:
        out.append((NT - i, S - P * i, P * i))
    return out


def step_uses(i):
    if i < STEPS - 1:
        return [[(h, kb, c, w) for kb, c, w in step_blocks(i)] for h in range(GH)]
    half = S // 2
    return [[(h, NT // 2, 0, half), (h + 1, NT // 2, half, half)] for h in range(0, GH, 2)]


ALL_STEPS = [(g, i) for g in range(NG) for i in range(STEPS)]


def ring_order():
    u = [(("xnT", 0), "act"), (("xnT", 1), "dve"), (("qkv", 0), "act"), (("qkv", 1), "act"),
         (("hidden", 0), "act"), (("qkv", 2), "act"), (("scores", 0), "dve")]
    for t in range(3, NT):
        u += [(("qkv", t), "act"), (("qT", t - 3), "act"), (("kT", t - 3), "dve"),
              (("mask", t - 3), "act"), (("mid", t - 3), "dve")]
    for t in range(NT - 3, NT):
        u += [(("qT", t), "act"), (("kT", t), "dve")]
        if t < NT - 1:
            u += [(("paths", t - NT + 3), "dve")]
    u += [(("max", (h, t)), "dve") for h in range(H) for t in range(NT)]
    u += [(("maxT", 0), "dve")]
    n = 0
    for s, (g, i) in enumerate(ALL_STEPS):
        for _ in step_uses(i):
            u.append((("S", n), "act"))
            n += 1
        if g and i == 2:
            u.append((("oT", g - 1), "dve"))
    u += [(("oT", NG - 1), "dve"), (("attnT", 0), "act"), (("attnT", 1), "dve"),
          (("proj", 0), "dve"), (("proj", 1), "dve")]
    return u


USES = ring_order()
NU = len(USES)
PLACE = {name: n for n, (name, _) in enumerate(USES)}
TAKER = dict(USES)
TAKEN = {}
for _who in ("act", "dve"):
    for _n, _name in enumerate([x for x, w in USES if w == _who]):
        TAKEN[_name] = _n + 1
NTAKEN = {w: sum(1 for _, x in USES if x == w) for w in ("act", "dve")}
NS = sum(len(step_uses(i)) for _, i in ALL_STEPS)
assert NU % 3 == 0 and NS % RING == 0
DVE_LINKS = 47


def build(nc, x, wqk, wv, wo, mixk, w1, b1, b1_last, w2, wo1, bo1, wo2, bo2, gamma, beta,
          cos_t, sin_t, ident, order, spread, out):
    ctx = ExitStack()
    with ctx:
        def sb(name, shape, dt):
            return ctx.enter_context(nc.sbuf_tensor(name, shape, dt))

        def sem(name):
            return ctx.enter_context(nc.semaphore(name))

        wqk_sb = sb("wqk_sb", [P, NC, 2 * D], F32)
        wv_sb = sb("wv_sb", [P, NC, D], F32)
        wo_sb = sb("wo_sb", [P, NC, D], F32)
        mixk_sb = sb("mixk_sb", [P, NC, 3], F32)
        w1_sb = sb("w1_sb", [P, NC, MID], F32)
        b1_sb = sb("b1_sb", [P, NJ], F32)
        w2_sb = sb("w2_sb", [P, NJ, D], F32)
        wo1_sb = sb("wo1_sb", [P, NC, DM], F32)
        bo1_sb = sb("bo1_sb", [DM, 1], F32)
        wo2_sb = sb("wo2_sb", [DM + 1, PATHS], F32)
        gamma_sb = sb("gamma_sb", [P, D], F32)
        beta_sb = sb("beta_sb", [P, D], F32)
        cos_sb = sb("cos_sb", [P, NT, DK], F32)
        sin_sb = sb("sin_sb", [P, NT, DK], F32)
        ident_sb = sb("ident_sb", [P, P], F32)
        ident_bf = sb("ident_bf", [P, P], BF16)
        causal_sb = sb("causal_sb", [P, S], BF16)
        order_sb = sb("order_sb", [P, PATHS], F32)
        xm = sb("xm", [P, NC, S], F32)
        spread_sb = xm[0:PATHS, 0, 0:MID + PATHS]
        spread_bf = sb("spread_bf", [PATHS, MID + PATHS], BF16)
        mhalf = sb("mhalf", [P, NT], F32)
        x_sb = sb("x_sb", [P, NT, D], F32)
        xn = sb("xn", [P, NT, D], F32)
        acc = sb("acc", [P, NT, D], F32)
        xnT = sb("xnT", [P, NC, S + 2], F32)
        attnT = xnT[:, :, 1:S + 1]
        attn = xm[:, :, :].rearrange("p c (t d) -> p (c t) d", d=D)
        stats = sb("stats", [P, NT, 6], F32)
        mv = sb("mv", [P, NT, 2], F32)
        ve = sb("ve", [P, NT], F32)
        rs = sb("rs", [P, NT], F32)
        rt = sb("rt", [P, NT], F32)
        hidden = sb("hidden", [DM + 1, S], F32)
        rmax = sb("rmax", [P, NT], F32)
        req = sb("req", [P, NT, PATHS], F32)
        onehot = sb("onehot", [P, NT, PATHS], BF16)
        onehotT = sb("onehotT", [PATHS, S], BF16)
        mask = sb("mask", [P, 2, S], BF16)
        q_sb = sb("q_sb", [P, 2, 2 * D], F32)
        rope_b = sb("rope_b", [P, 2, 2 * D], F32)
        roped = sb("roped", [P, 2, 2 * D], F32)
        rest = sb("rest", [P, 2 * D], F32)
        v_sb = sb("v_sb", [P, NT, H, VW], F32)
        qT = sb("qT", [PARTS + SHIFT, H, S], BF16)
        kT = sb("kT", [PARTS + SHIFT, H, S], BF16)
        rowmax = sb("rowmax", [P, NT, H], F32)
        shift_hi = mask[0:H, 0, :]
        shift_lo = mask[0:H, 1, :]
        prob = sb("prob", [P, RING, S], F32)
        mid = prob[:, 0:NJ, :]
        parts = prob[:, NJ:RING, :].rearrange("p r s -> p (r s)").bitcast(BF16).rearrange(
            "p (i a h n) -> p i a h n", i=2, a=2, h=H)
        o_sb = sb("o_sb", [P, S], F32)
        shift_f = o_sb[0:H, :]
        rden = sb("rden", [P, NT, GH], F32)
        slots = [ctx.enter_context(nc.psum_tensor(f"slot{i}", [P, SLOT], F32)) for i in range(3)]
        o_ps = ctx.enter_context(nc.psum_tensor("o_ps", [P, SLOT], F32))

        weights_loaded = sem("weights_loaded")
        consts_set = sem("consts_set")
        gates_passed = sem("gates_passed")
        ones_set = sem("ones_set")
        x_loaded = sem("x_loaded")
        slot_filled = sem("slot_filled")
        act_took = sem("act_took")
        dve_took = sem("dve_took")
        dve_linked = sem("dve_linked")
        var_ready = sem("var_ready")
        rsqrt_ready = sem("rsqrt_ready")
        xn_ready = sem("xn_ready")
        acc_begun = sem("acc_begun")
        acc_ffn = sem("acc_ffn")
        mixed = sem("mixed")
        routed = sem("routed")
        onehot_turned = sem("onehot_turned")
        onehot_ready = sem("onehot_ready")
        rope_swapped = sem("rope_swapped")
        rope_done = sem("rope_done")
        hi_cut = sem("hi_cut")
        all_cut = sem("all_cut")
        mid_ready = sem("mid_ready")
        normed = sem("normed")
        shift_ready = sem("shift_ready")
        shift_placed = sem("shift_placed")
        masked = sem("masked")
        pv_done = sem("pv_done")
        o_copied = sem("o_copied")
        out_ready = sem("out_ready")
        out_stored = sem("out_stored")
        slot_reads = {"act": act_took, "dve": dve_took}

        NWEIGHTS = 20
        NCONSTS = 8

        def gate(eng):
            eng.sem_inc(gates_passed, 1)

        def now(b, per, k):
            return b * per + k

        def filled(b, name):
            return b * NU + PLACE[name] + 1

        def took(b, name):
            return (b + 1) * NTAKEN[TAKER[name]] + TAKEN[name]

        def slot_of(name):
            return slots[PLACE[name] % 3]

        block = ctx.enter_context(nc.Block())

        @block.sync
        def _(sp):
            def load_x(b):
                sp.dma_start(x_sb[:, :, :], x[bass.ds(b, 1)].rearrange("a (t p) d -> p (a t) d", p=P)
                             ).then_inc(x_loaded, 16)

            load_x(0)
            sp.dma_start(ident_sb[:, :], ident).then_inc(weights_loaded, 16)
            sp.dma_start(gamma_sb[:, :], gamma.partition_broadcast(P)).then_inc(weights_loaded, 16)
            sp.dma_start(beta_sb[:, :], beta.partition_broadcast(P)).then_inc(weights_loaded, 16)
            for dst, src in ((mixk_sb, mixk), (wqk_sb, wqk), (wv_sb, wv), (wo1_sb, wo1),
                             (cos_sb, cos_t), (sin_sb, sin_t), (w1_sb, w1), (wo_sb, wo)):
                sp.dma_start(dst[:, :, :], src).then_inc(weights_loaded, 16)
            sp.dma_start(bo1_sb[:, :], bo1).then_inc(weights_loaded, 16)
            sp.dma_start(wo2_sb[0:DM, :], wo2).then_inc(weights_loaded, 16)
            sp.dma_start(wo2_sb[DM:DM + 1, :], bo2).then_inc(weights_loaded, 16)
            sp.dma_start(b1_sb[:, 0:NJ - 1], b1).then_inc(weights_loaded, 16)
            sp.dma_start(b1_sb[0:DM, NJ - 1:NJ], b1_last).then_inc(weights_loaded, 16)
            sp.dma_start(w2_sb[:, 0:NJ - 1, :], w2[0:P * (NJ - 1)].rearrange("(j p) d -> p j d", p=P)
                         ).then_inc(weights_loaded, 16)
            sp.dma_start(w2_sb[0:LAST, NJ - 1, :], w2[P * (NJ - 1):MID + PATHS]).then_inc(weights_loaded, 16)
            sp.dma_start(spread_sb, spread).then_inc(weights_loaded, 16)
            sp.dma_start(order_sb[:, :], order).then_inc(weights_loaded, 16)

            def place_shift(b):
                sp.wait_ge(shift_ready, now(b, 1, 1))
                sp.dma_start(qT[PARTS:PARTS + 1, :, :], shift_hi[:, :]).then_inc(shift_placed, 16)
                sp.dma_start(qT[PARTS + 1:PARTS + 2, :, :], shift_lo[:, :]).then_inc(shift_placed, 16)

            def store(b):
                for i in range(2):
                    sp.wait_ge(out_ready, now(b, 2, i + 1))
                    sp.dma_start(out[bass.ds(b, 1), i * S // 2:(i + 1) * S // 2, :]
                                 .rearrange("a (t p) d -> p (a t) d", p=P),
                                 acc[:, i * NT // 2:(i + 1) * NT // 2, :]).then_inc(out_stored, 16)

            with sp.Fori(0, B - 1) as b:
                place_shift(b)
                sp.wait_ge(xn_ready, now(b, NT, NT))
                sp.wait_ge(acc_begun, now(b, 1, 1))
                load_x(b + 1)
                store(b)
            place_shift(B - 1)
            store(B - 1)
            sp.wait_ge(out_stored, 32 * B + 32)

        @block.gpsimd
        def _(pool):
            made = [0]

            def make(ins):
                made[0] += 1
                ins.then_inc(consts_set, 1)
                pool.wait_ge(consts_set, made[0])

            make(nc.gpsimd.memset(xnT[:, :, :], 0.0))
            make(nc.gpsimd.memset(v_sb[:, :, :, :], 0.0))
            make(nc.gpsimd.memset(v_sb[:, :, :, DK:DK + 1], 1.0))
            make(nc.gpsimd.memset(mhalf[:, :], -0.5))
            make(nc.gpsimd.memset(causal_sb[:, :], 0.0))
            make(nc.gpsimd.affine_select(out=causal_sb[:, S - P:], in_=causal_sb[:, S - P:],
                                         compare_op=ALU.is_ge, fill=NEG, base=0, pattern=[[-1, P]],
                                         channel_multiplier=1))
            pool.wait_ge(weights_loaded, 16 * NWEIGHTS)
            make(nc.gpsimd.tensor_copy(ident_bf[:, :], ident_sb[:, :]))
            make(nc.gpsimd.tensor_copy(spread_bf[:, :], spread_sb))
            assert made[0] == NCONSTS
            pool.sem_inc(out_stored, 32)

            with pool.Fori(0, B) as b:
                def rsqrt(n):
                    pool.wait_ge(var_ready, now(b, 2, n))
                    nc.gpsimd.tensor_tensor(rs[:, :], ve[:, :], mhalf[:, :], ALU.pow).then_inc(rsqrt_ready, 1)

                rsqrt(1)
                pool.wait_ge(out_stored, now(b, 32, 32))
                nc.gpsimd.tensor_tensor(acc[:, :, :], x_sb[:, :, :],
                                        beta_sb[:, None, :].to_broadcast([P, NT, D]),
                                        ALU.add).then_inc(acc_begun, 1)
                for t in range(NT):
                    pool.wait_ge(act_took, took(b, ("qkv", t)))
                    if t >= 2:
                        pool.wait_ge(rope_done, now(b, NT, t - 1))
                    q4 = q_sb[:, t % 2, :].rearrange("p (h d) -> p h d", d=DK)
                    r4 = rope_b[:, t % 2, :].rearrange("p (h d) -> p h d", d=DK)
                    hd = DK // 2
                    for a, z in ((0, hd), (hd, 0)):
                        ins = nc.gpsimd.tensor_tensor(
                            r4[:, :, a:a + hd], q4[:, :, z:z + hd],
                            sin_sb[:, t, None, a:a + hd].to_broadcast([P, 2 * H, hd]), ALU.mult)
                    ins.then_inc(rope_swapped, 1)
                rsqrt(2)
                for i in range(2):
                    pool.wait_ge(normed, now(b, 2, i + 1))
                    y = xn[:, i * NT // 2:(i + 1) * NT // 2, :]
                    a = acc[:, i * NT // 2:(i + 1) * NT // 2, :]
                    nc.gpsimd.tensor_tensor(y, y, gamma_sb[:, None, :].to_broadcast([P, NT // 2, D]),
                                            ALU.mult).then_inc(acc_ffn, 1)
                    pool.wait_ge(acc_ffn, now(b, 4, 2 * i + 1))
                    nc.gpsimd.tensor_tensor(a, a, y, ALU.add).then_inc(acc_ffn, 1)
                n = 0
                for g, i in ALL_STEPS:
                    for blocks in step_uses(i):
                        pool.wait_ge(act_took, took(b, ("S", n)))
                        gate(pool)
                        for k, (_, _, c, _) in enumerate(blocks):
                            d = prob[:, n % RING, c:c + P]
                            ins = nc.gpsimd.affine_select(out=d, in_=d, compare_op=ALU.is_ge, fill=0.0, base=0,
                                                          pattern=[[1, P]], channel_multiplier=-1)
                        ins.then_inc(masked, 1)
                        n += 1

        @block.scalar
        def _(act):
            act.sem_inc(act_took, NTAKEN["act"])
            with act.Fori(0, B) as b:
                def take(name):
                    act.wait_ge(slot_filled, filled(b, name))
                    return slot_of(name)

                def copy_qkv(t):
                    if t >= 2:
                        act.wait_ge(rope_done, now(b, NT, t - 1))
                    ps = take(("qkv", t))
                    nc.scalar.copy(q_sb[:, t % 2, :], ps[:, 0:2 * D])
                    nc.scalar.copy(v_sb[:, t, :, 0:DK],
                                   ps[:, 2 * D:3 * D].rearrange("p (h d) -> p h d", d=DK)
                                   ).then_inc(act_took, 1)

                def cut_hi(t):
                    act.wait_ge(rope_done, now(b, NT, t + 1))
                    if t >= 2:
                        act.wait_ge(slot_filled, filled(b, ("kT", t - 2)))
                    pt = parts[:, t % 2, :, :, :].rearrange("p a h (n d) -> p a h n d", d=DK)
                    r = roped[:, t % 2, :].rearrange("p (a h d) -> p a h d", a=2, d=DK)
                    nc.scalar.copy(pt[:, 0, :, 0:6:3, :], r[:, 0, :, None, :].to_broadcast([P, H, 2, DK]))
                    nc.scalar.copy(pt[:, 0, :, 5, :], r[:, 0, :, :])
                    nc.scalar.copy(pt[:, 1, :, 0:3, :], r[:, 1, :, None, :].to_broadcast([P, H, 3, DK])
                                   ).then_inc(hi_cut, 1)

                def copy_qT(t):
                    ps = take(("qT", t))
                    nc.scalar.copy(qT[0:PARTS, :, t * P:(t + 1) * P],
                                   ps[0:PARTS, :].bitcast(BF16).rearrange("p (h c) -> p h c", c=P)
                                   ).then_inc(act_took, 1)

                def copy_mask(j):
                    if j >= 2:
                        act.wait_ge(dve_took, took(b, ("mid", j - 2)))
                    ps = take(("mask", j))
                    rows = P if j < NJ - 1 else LAST
                    nc.scalar.copy(mask[0:rows, j % 2, :], ps[0:rows, :]).then_inc(act_took, 1)

                ps = take(("xnT", 0))
                nc.scalar.copy(xnT[:, 0, 1:S + 1], ps[:, :]).then_inc(act_took, 1)
                copy_qkv(0)
                copy_qkv(1)
                cut_hi(0)
                ps = take(("hidden", 0))
                nc.scalar.activation(hidden[0:DM, :], ps[0:DM, :], ACT.Tanh,
                                     bias=bo1_sb[:, 0:1]).then_inc(act_took, 1)
                copy_qkv(2)
                cut_hi(1)
                for t in range(3, NT):
                    copy_qkv(t)
                    cut_hi(t - 1)
                    copy_qT(t - 3)
                    copy_mask(t - 3)
                cut_hi(NT - 1)
                for t in range(NT - 3, NT):
                    copy_qT(t)
                for n in range(NS):
                    if n >= RING:
                        act.wait_ge(pv_done, now(b, len(ALL_STEPS), step_of(n - RING) + 1))
                    ps = take(("S", n))
                    nc.scalar.activation(prob[:, n % RING, :], ps[:, :], ACT.Exp,
                                         scale=float(DK) ** -0.5).then_inc(act_took, 1)
                ps = take(("attnT", 0))
                nc.scalar.copy(attnT[:, 0, :], ps[:, :]).then_inc(act_took, 1)

        @block.vector
        def _(dve):
            dve.sem_inc(dve_took, NTAKEN["dve"])
            nc.vector.memset(kT[PARTS:PARTS + SHIFT, :, :], 1.0).then_inc(ones_set, 1)
            nc.vector.memset(hidden[DM:DM + 1, :], 1.0).then_inc(ones_set, 1)
            dve.wait_ge(weights_loaded, 16 * NWEIGHTS)
            dve.wait_ge(consts_set, NCONSTS)
            with dve.Fori(0, B) as b:
                links = [0]

                def link(ins):
                    links[0] += 1
                    ins.then_inc(dve_linked, 1)
                    dve.wait_ge(dve_linked, now(b, DVE_LINKS, links[0]))

                def take(name):
                    dve.wait_ge(slot_filled, filled(b, name))
                    return slot_of(name)

                def norm_stats(src, n):
                    for t in range(NT):
                        ins = nc.vector.bn_stats(stats[:, t, :], src[:, t, :])
                    link(ins)
                    gate(dve)
                    for t in range(NT):
                        ins = nc.vector.bn_aggr(mv[:, t, :], stats[:, t, :])
                    link(ins)
                    nc.vector.tensor_scalar(ve[:, :], mv[:, :, 1], EPS, None, ALU.add).then_inc(var_ready, 1)
                    dve.wait_ge(rsqrt_ready, now(b, 2, n))
                    link(nc.vector.tensor_tensor(rt[:, :], rs[:, :], rs[:, :], ALU.mult))
                    link(nc.vector.tensor_tensor(rt[:, :], rt[:, :], ve[:, :], ALU.mult))
                    link(nc.vector.tensor_scalar(rt[:, :], rt[:, :], -0.5, 1.5, ALU.mult, ALU.add))
                    link(nc.vector.tensor_tensor(rt[:, :], rs[:, :], rt[:, :], ALU.mult))

                def normalize(dst, src, t):
                    return nc.vector.tensor_scalar(dst[:, t, :], src[:, t, :], mv[:, t, 0:1], rt[:, t:t + 1],
                                                   ALU.subtract, ALU.mult)

                def rotate(t):
                    dve.wait_ge(act_took, took(b, ("qkv", t)))
                    if t >= 2:
                        dve.wait_ge(hi_cut, now(b, NT, t - 1))
                    link(nc.vector.tensor_tensor(
                        roped[:, t % 2, :].rearrange("p (h d) -> p h d", d=DK),
                        q_sb[:, t % 2, :].rearrange("p (h d) -> p h d", d=DK),
                        cos_sb[:, t, None, :].to_broadcast([P, 2 * H, DK]), ALU.mult))
                    dve.wait_ge(rope_swapped, now(b, NT, t + 1))
                    nc.vector.tensor_tensor(roped[:, t % 2, :], roped[:, t % 2, :], rope_b[:, t % 2, :],
                                            ALU.add).then_inc(rope_done, 1)

                def cut_rest(t):
                    dve.wait_ge(hi_cut, now(b, NT, t + 1))
                    pt = parts[:, t % 2, :, :, :].rearrange("p a h (n d) -> p a h n d", d=DK)
                    r = roped[:, t % 2, :].rearrange("p (a h d) -> p a h d", a=2, d=DK)
                    e = rest[:, :].rearrange("p (a h d) -> p a h d", a=2, d=DK)
                    link(nc.vector.tensor_tensor(e, r, pt[:, :, :, 0, :], ALU.subtract))
                    nc.vector.tensor_copy(pt[:, 0, :, 1:5:3, :], e[:, 0, :, None, :].to_broadcast([P, H, 2, DK]))
                    link(nc.vector.tensor_copy(pt[:, 1, :, 3:5, :],
                                               e[:, 1, :, None, :].to_broadcast([P, H, 2, DK])))
                    nc.vector.tensor_tensor(pt[:, 0, :, 2, :], e[:, 0], pt[:, 0, :, 1, :], ALU.subtract)
                    nc.vector.tensor_tensor(pt[:, 1, :, 5, :], e[:, 1], pt[:, 1, :, 3, :],
                                            ALU.subtract).then_inc(all_cut, 1)

                def copy_kT(t):
                    ps = take(("kT", t))
                    nc.vector.tensor_copy(kT[0:PARTS, :, t * P:(t + 1) * P],
                                          ps[0:PARTS, :].bitcast(BF16).rearrange("p (h c) -> p h c", c=P)
                                          ).then_inc(dve_took, 1)

                def route():
                    ps = take(("scores", 0))
                    sc = ps[:, 0:NT * PATHS].rearrange("p (t n) -> p t n", n=PATHS)
                    link(nc.vector.tensor_reduce(rmax[:, :], sc, AX.X, ALU.max))
                    nc.vector.tensor_tensor(req[:, :, :], sc, rmax[:, :, None].to_broadcast([P, NT, PATHS]),
                                            ALU.is_equal).then_inc(dve_took, 1)
                    dve.wait_ge(dve_took, took(b, ("scores", 0)))
                    link(nc.vector.tensor_tensor(req[:, :, :], req[:, :, :],
                                                 order_sb[:, None, :].to_broadcast([P, NT, PATHS]), ALU.mult))
                    link(nc.vector.tensor_reduce(rmax[:, :], req[:, :, :], AX.X, ALU.max))
                    nc.vector.tensor_tensor(onehot[:, :, :], req[:, :, :],
                                            rmax[:, :, None].to_broadcast([P, NT, PATHS]),
                                            ALU.is_equal).then_inc(routed, 1)

                def copy_onehotT():
                    dve.wait_ge(onehot_turned, now(b, 1, 1))
                    nc.vector.tensor_copy(onehotT[:, :], o_ps[0:PATHS, 0:S // 2].bitcast(BF16)
                                          ).then_inc(onehot_ready, 1)

                def select_mid(j):
                    dve.wait_ge(act_took, took(b, ("mask", j)))
                    rows = P if j < NJ - 1 else DM
                    if j == NJ - 1:
                        nc.vector.tensor_copy(mid[DM:LAST, j, :], mask[DM:LAST, j % 2, :])
                    ps = take(("mid", j))
                    nc.vector.scalar_tensor_tensor(mid[0:rows, j, :], ps[0:rows, :], b1_sb[0:rows, j:j + 1],
                                                   mask[0:rows, j % 2, :], ALU.add, ALU.mult
                                                   ).then_inc(dve_took, 1)

                def add_paths(i):
                    ps = take(("paths", i))
                    y = xn[:, i * NT // 2:(i + 1) * NT // 2, :]
                    nc.vector.tensor_tensor(y, ps[:, :].rearrange("p (t d) -> p t d", d=D), y,
                                            ALU.add).then_inc(dve_took, 1)

                dve.wait_ge(x_loaded, now(b, 16, 16))
                norm_stats(x_sb, 1)
                for t in range(NT):
                    normalize(xn, x_sb, t).then_inc(xn_ready, 1)
                ps = take(("xnT", 1))
                nc.vector.tensor_copy(xnT[:, 1, 1:S + 1], ps[:, :]).then_inc(dve_took, 1)
                dve.wait_ge(act_took, took(b, ("xnT", 0)))
                dve.wait_ge(dve_took, took(b, ("xnT", 1)))
                for k in range(3):
                    for c in range(NC):
                        if k == 0:
                            ins = nc.vector.tensor_scalar(xm[:, c, :], xnT[:, c, 0:S], mixk_sb[:, c, 0:1],
                                                          None, ALU.mult)
                        else:
                            ins = nc.vector.scalar_tensor_tensor(xm[:, c, :], xnT[:, c, k:k + S],
                                                                 mixk_sb[:, c, k:k + 1], xm[:, c, :],
                                                                 ALU.mult, ALU.add)
                    if k < 2:
                        link(ins)
                ins.then_inc(mixed, 1)
                rotate(0)
                rotate(1)
                cut_rest(0)
                route()
                rotate(2)
                cut_rest(1)
                for t in range(3, NT):
                    rotate(t)
                    if t == 3:
                        copy_onehotT()
                    cut_rest(t - 1)
                    copy_kT(t - 3)
                    select_mid(t - 3)
                cut_rest(NT - 1)
                for t in range(NT - 3, NT):
                    copy_kT(t)
                    if t < NT - 1:
                        add_paths(t - NT + 3)
                dve.wait_ge(dve_took, took(b, ("paths", 1)))
                norm_stats(xn, 2)
                for t in range(NT):
                    ins = normalize(xn, xn, t)
                    if t % (NT // 2) == NT // 2 - 1:
                        ins.then_inc(normed, 1)
                for h in range(H):
                    for t in range(NT):
                        ps = take(("max", (h, t)))
                        gate(dve)
                        w = (t + 1) * P
                        nc.vector.tensor_tensor_reduce(ps[:, 0:w], ps[:, 0:w], causal_sb[:, S - w:S],
                                                       1.0, NEG, ALU.add, ALU.max,
                                                       rowmax[:, t, h:h + 1]).then_inc(dve_took, 1)
                ps = take(("maxT", 0))
                link(nc.vector.tensor_scalar(shift_f[:, :], ps[0:H, :], -1.0, None, ALU.mult))
                link(nc.vector.tensor_copy(shift_hi[:, :], shift_f[:, :]))
                nc.vector.tensor_tensor(shift_lo[:, :], shift_f[:, :], shift_hi[:, :],
                                        ALU.subtract).then_inc(shift_ready, 1)
                nc.vector.tensor_copy(rmax[0:1, 0:1], ps[0:1, 0:1]).then_inc(dve_took, 1)
                for g in range(NG):
                    dve.wait_ge(pv_done, now(b, len(ALL_STEPS), STEPS * (g + 1)))
                    if g:
                        dve.wait_ge(slot_filled, filled(b, ("oT", g - 1)))
                    nc.vector.tensor_copy(o_sb[:, :], o_ps[:, :]).then_inc(o_copied, 1)
                    ps = take(("oT", g))
                    o4 = ps[:, :].rearrange("p (t h v) -> p t h v", h=GH, v=VW)
                    link(nc.vector.reciprocal(rden[:, :, :], o4[:, :, :, DK]))
                    nc.vector.tensor_tensor(
                        attn[:, :, g * GH * DK:(g + 1) * GH * DK].rearrange("p t (h d) -> p t h d", d=DK),
                        o4[:, :, :, 0:DK], rden[:, :, :, None].to_broadcast([P, NT, GH, DK]),
                        ALU.mult).then_inc(dve_took, 1)
                ps = take(("attnT", 1))
                nc.vector.tensor_copy(attnT[:, 1, :], ps[:, :]).then_inc(dve_took, 1)
                dve.wait_ge(acc_ffn, now(b, 4, 4))
                for i in range(2):
                    ps = take(("proj", i))
                    a = acc[:, i * NT // 2:(i + 1) * NT // 2, :]
                    nc.vector.tensor_tensor(a, ps[:, :].rearrange("p (t d) -> p t d", d=D), a,
                                            ALU.add).then_inc(dve_took, 1)
                    dve.wait_ge(dve_took, took(b, ("proj", i)))
                    nc.vector.tensor_copy(rmax[0:1, 0:1], acc[0:1, i * NT // 2, 0:1]).then_inc(out_ready, 1)
                assert links[0] == DVE_LINKS, links[0]

        @block.tensor
        def _(pe):
            pe.wait_ge(weights_loaded, 16 * NWEIGHTS)
            pe.wait_ge(consts_set, NCONSTS)
            pe.wait_ge(ones_set, 2)
            with pe.Fori(0, B) as b:
                def begin(name):
                    u = PLACE[name]
                    old = USES[(u - 3) % NU][0]
                    who = TAKER[old]
                    value = b * NTAKEN[who] + TAKEN[old] + (NTAKEN[who] if u >= 3 else 0)
                    pe.wait_ge(slot_reads[who], value)
                    return slot_of(name)

                def turn(name, src, chunk):
                    ps = begin(name)
                    for t in range(NT):
                        ins = nc.tensor.transpose(ps[:, t * P:(t + 1) * P], src[:, t, chunk * P:(chunk + 1) * P],
                                                  ident_sb[:, :])
                    ins.then_inc(slot_filled, 1)

                def project(t):
                    ps = begin(("qkv", t))
                    if t == 0:
                        pe.wait_ge(act_took, took(b, ("xnT", 0)))
                        pe.wait_ge(dve_took, took(b, ("xnT", 1)))
                    for w, a, n in ((wqk_sb, 0, 2 * D), (wv_sb, 2 * D, D)):
                        for c in range(NC):
                            ins = nc.tensor.matmul(ps[:, a:a + n], xnT[:, c, 1 + t * P:1 + (t + 1) * P], w[:, c, :],
                                                   start=(c == 0), stop=(c == NC - 1))
                    ins.then_inc(slot_filled, 1)

                def router_hidden():
                    ps = begin(("hidden", 0))
                    pe.wait_ge(mixed, now(b, 1, 1))
                    for n in range(0, S, 512):
                        for c in range(NC):
                            ins = nc.tensor.matmul(ps[0:DM, n:n + 512], wo1_sb[:, c, :], xm[:, c, n:n + 512],
                                                   start=(c == 0), stop=(c == NC - 1))
                    ins.then_inc(slot_filled, 1)

                def router_scores():
                    ps = begin(("scores", 0))
                    pe.wait_ge(act_took, took(b, ("hidden", 0)))
                    for t in range(NT):
                        ins = nc.tensor.matmul(ps[:, t * PATHS:(t + 1) * PATHS], hidden[:, t * P:(t + 1) * P],
                                               wo2_sb[:, :], start=True, stop=True)
                    ins.then_inc(slot_filled, 1)

                def turn_parts(t):
                    for a, name in enumerate(("qT", "kT")):
                        ps = begin((name, t))
                        if a == 0:
                            pe.wait_ge(all_cut, now(b, NT, t + 1))
                        view = ps[0:PARTS, :].bitcast(BF16)
                        for h in range(H):
                            ins = nc.tensor.transpose(view[:, h * P:(h + 1) * P], parts[:, t % 2, a, h, :],
                                                      ident_bf[:, :])
                        ins.then_inc(slot_filled, 1)

                def turn_onehot():
                    pe.wait_ge(routed, now(b, 1, 1))
                    view = o_ps[0:PATHS, 0:S // 2].bitcast(BF16)
                    for t in range(NT):
                        ins = nc.tensor.transpose(view[:, t * P:(t + 1) * P], onehot[:, t, :], ident_bf[:, :])
                    ins.then_inc(onehot_turned, 1)

                def spread_mask(j):
                    ps = begin(("mask", j))
                    if j == 0:
                        pe.wait_ge(onehot_ready, now(b, 1, 1))
                    rows = P if j < NJ - 1 else LAST
                    for n in range(0, S, 512):
                        ins = nc.tensor.matmul(ps[0:rows, n:n + 512], spread_bf[:, j * P:j * P + rows],
                                               onehotT[:, n:n + 512], start=True, stop=True)
                    ins.then_inc(slot_filled, 1)

                def middle(j):
                    ps = begin(("mid", j))
                    rows = P if j < NJ - 1 else DM
                    for n in range(0, S, 512):
                        for c in range(NC):
                            ins = nc.tensor.matmul(ps[0:rows, n:n + 512], w1_sb[:, c, j * P:j * P + rows],
                                                   xm[:, c, n:n + 512], start=(c == 0), stop=(c == NC - 1))
                    ins.then_inc(slot_filled, 1)

                def paths_out(i):
                    ps = begin(("paths", i))
                    if i == 0:
                        pe.wait_ge(dve_took, took(b, ("mid", NJ - 1)))
                    for k in range(NT // 2):
                        t = i * NT // 2 + k
                        for j in range(NJ):
                            rows = P if j < NJ - 1 else LAST
                            ins = nc.tensor.matmul(ps[:, k * D:(k + 1) * D], mid[0:rows, j, t * P:(t + 1) * P],
                                                   w2_sb[0:rows, j, :], start=(j == 0), stop=(j == NJ - 1))
                    ins.then_inc(slot_filled, 1)

                def max_scores(h, t):
                    ps = begin(("max", (h, t)))
                    for n in range(0, (t + 1) * P, 512):
                        w = min(512, (t + 1) * P - n)
                        ins = nc.tensor.matmul(ps[:, n:n + w], qT[0:PARTS, h, t * P:(t + 1) * P],
                                               kT[0:PARTS, h, n:n + w], start=True, stop=True)
                    ins.then_inc(slot_filled, 1)

                def score(n, g, blocks):
                    ps = begin(("S", n))
                    for hh, kb, c0, w in blocks:
                        h = g * GH + hh
                        c = c0
                        while c < c0 + w:
                            e = min(c0 + w, (c // 512 + 1) * 512)
                            q = kb * P + c - c0
                            ins = nc.tensor.matmul(ps[:, c:e], kT[:, h, kb * P:(kb + 1) * P],
                                                   qT[:, h, q:q + e - c], start=True, stop=True)
                            c = e
                    ins.then_inc(slot_filled, 1)

                def values(s, n0):
                    g, i = ALL_STEPS[s]
                    uses = step_uses(i)
                    pe.wait_ge(masked, now(b, NS, n0 + len(uses)))
                    if g and i == 0:
                        pe.wait_ge(o_copied, now(b, NG, g))
                    todo = []
                    for k, blocks in enumerate(uses):
                        for hh, kb, c0, w in blocks:
                            q = kb * P
                            while q < S:
                                e = (q // 512 + 1) * 512
                                todo.append((kb, q, e, hh, k, c0 + q - kb * P))
                                q = e
                    todo.sort(key=lambda m: (m[0], m[1], m[3]))
                    for kb, q, e, hh, k, c in todo:
                        h = g * GH + hh
                        last = (kb == NT // 2) if q >= 512 else (kb == NT // 2 - 1)
                        ins = nc.tensor.matmul(o_ps[VW * hh:VW * (hh + 1), q:e],
                                               v_sb[:, kb, h, :],
                                               prob[:, (n0 + k) % RING, c:c + e - q],
                                               start=(kb == 0), stop=last)
                    ins.then_inc(pv_done, 1)

                def turn_sums(g):
                    ps = begin(("oT", g))
                    pe.wait_ge(o_copied, now(b, NG, g + 1))
                    for t in range(NT):
                        ins = nc.tensor.transpose(ps[:, t * P:(t + 1) * P], o_sb[:, t * P:(t + 1) * P],
                                                  ident_sb[:, :])
                    ins.then_inc(slot_filled, 1)

                def out_project(i):
                    ps = begin(("proj", i))
                    if i == 0:
                        pe.wait_ge(act_took, took(b, ("attnT", 0)))
                        pe.wait_ge(dve_took, took(b, ("attnT", 1)))
                    for k in range(NT // 2):
                        t = i * NT // 2 + k
                        for c in range(NC):
                            ins = nc.tensor.matmul(ps[:, k * D:(k + 1) * D], attnT[:, c, t * P:(t + 1) * P],
                                                   wo_sb[:, c, :], start=(c == 0), stop=(c == NC - 1))
                    ins.then_inc(slot_filled, 1)

                pe.wait_ge(xn_ready, now(b, NT, NT))
                turn(("xnT", 0), xn, 0)
                turn(("xnT", 1), xn, 1)
                project(0)
                project(1)
                router_hidden()
                project(2)
                router_scores()
                for t in range(3, NT):
                    project(t)
                    if t == 3:
                        turn_onehot()
                    turn_parts(t - 3)
                    spread_mask(t - 3)
                    middle(t - 3)
                for t in range(NT - 3, NT):
                    turn_parts(t)
                    if t < NT - 1:
                        paths_out(t - NT + 3)

                pe.wait_ge(act_took, took(b, ("qT", NT - 1)))
                pe.wait_ge(dve_took, took(b, ("kT", NT - 1)))
                for h in range(H):
                    for t in range(NT):
                        max_scores(h, t)
                ps = begin(("maxT", 0))
                pe.wait_ge(dve_took, took(b, ("max", (H - 1, NT - 1))))
                for t in range(NT):
                    ins = nc.tensor.transpose(ps[0:H, t * P:(t + 1) * P], rowmax[:, t, :], ident_sb[:, :])
                ins.then_inc(slot_filled, 1)

                pe.wait_ge(shift_placed, now(b, 32, 32))
                n = 0
                starts = []
                for s, (g, i) in enumerate(ALL_STEPS):
                    starts.append(n)
                    uses = step_uses(i)
                    for k, blocks in enumerate(uses):
                        if k == 3 and s:
                            values(s - 1, starts[s - 1])
                        score(n, g, blocks)
                        n += 1
                    if len(uses) < 4:
                        values(s - 1, starts[s - 1])
                    if g and i == 2:
                        turn_sums(g - 1)
                values(len(ALL_STEPS) - 1, starts[-1])
                turn_sums(NG - 1)
                pe.wait_ge(dve_took, took(b, ("oT", NG - 1)))
                turn(("attnT", 0), attn, 0)
                turn(("attnT", 1), attn, 1)
                out_project(0)
                out_project(1)


def step_of(n):
    for s, (_, i) in enumerate(ALL_STEPS):
        n -= len(step_uses(i))
        if n < 0:
            return s


def kernel(**inputs):
    import numpy as _np
    import concourse.bacc as _bacc
    from concourse import mybir as _mybir
    from concourse.bass_utils import run_bass_kernel_spmd as _run

    a = {k: _np.asarray(v) for k, v in inputs.items()}

    def chunks(w):
        return w.reshape(w.shape[0] // P, P, w.shape[1]).transpose(1, 0, 2)

    pair = _np.concatenate([_np.arange(0, DK, 2), _np.arange(1, DK, 2)])
    rows = (_np.arange(H)[:, None] * DK + pair[None, :]).reshape(-1)
    wqk = _np.concatenate([a["L0_attn_Wq"][rows], a["L0_attn_Wk"][rows]], axis=0).T
    w2 = _np.concatenate([a["L0_ffn_W2"].reshape(MID, D), a["L0_ffn_b2"]], axis=0)

    rates = _np.float32(THETA) ** (-(_np.float32(2.0) * _np.arange(DK // 2, dtype=_np.float32)) / _np.float32(DK))
    angle = _np.arange(S, dtype=_np.float32)[:, None] * rates[None, :].astype(_np.float32)
    cos, sin = _np.cos(angle), _np.sin(angle)
    cos_t = _np.concatenate([cos, cos], axis=1).astype(_np.float32)
    sin_t = _np.concatenate([-sin, sin], axis=1).astype(_np.float32)

    spread = _np.concatenate([_np.repeat(_np.eye(PATHS), DM, axis=1), _np.eye(PATHS)], axis=1)

    sent = {
        "x": a["L0_attn_x"],
        "wqk": chunks(wqk),
        "wv": chunks(a["L0_attn_Wv"].T),
        "wo": chunks(a["L0_attn_Wo"].T),
        "mixk": chunks(a["L0_ffn_mix_kernel"].T),
        "w1": chunks(a["L0_ffn_W1"].transpose(1, 0, 2).reshape(D, MID)),
        "b1": a["L0_ffn_b1"].reshape(MID)[:P * (NJ - 1)].reshape(NJ - 1, P).T,
        "b1_last": a["L0_ffn_b1"][PATHS - 1].reshape(DM, 1),
        "w2": w2,
        "wo1": chunks(a["L0_ffn_Wo1"]),
        "bo1": a["L0_ffn_bo1"].reshape(DM, 1),
        "wo2": a["L0_ffn_Wo2"],
        "bo2": a["L0_ffn_bo2"].reshape(1, PATHS),
        "gamma": a["L0_ffn_gamma"],
        "beta": a["L0_ffn_beta"],
        "cos_t": chunks(cos_t),
        "sin_t": chunks(sin_t),
        "ident": _np.eye(P, dtype=_np.float32),
        "spread": spread.astype(_np.float32),
        "order": _np.tile(_np.arange(PATHS, 0, -1, dtype=_np.float32), (P, 1)),
    }
    nc = _bacc.Bacc("TRN2", target_bir_lowering=False, num_devices=1)
    arrays, args = {}, {}
    for name, v in sent.items():
        v = _np.ascontiguousarray(v)
        arrays[f"in_{name}"] = v
        args[name] = nc.dram_tensor(f"in_{name}", v.shape, _mybir.dt.from_np(v.dtype), kind="ExternalInput").ap()
    args["out"] = nc.dram_tensor("out_0", (B, S, D), F32, kind="ExternalOutput").ap()
    build(nc, **args)
    r = _run(nc, [arrays], core_ids=[0])
    return r.results[0]["out_0"]
```

```python
from contextlib import ExitStack

import concourse.bass as bass
from concourse import mybir

ALU = mybir.AluOpType
ACT = mybir.ActivationFunctionType
AX = mybir.AxisListType
BF16 = mybir.dt.bfloat16
F32 = mybir.dt.float32

B, S, D = 4, 1024, 256
H = 16
DK = D // H
P = 128
NT = S // P
NC = D // P
PATHS = 9
DM = D // 4
MID = PATHS * DM
NJ = (MID + P - 1) // P
LAST = DM + PATHS
PARTS = 6 * DK
SHIFT = 2
VW = 32
GH = 4
NG = H // GH
RING = 8
SLOT = 1024
EPS = 1e-5
THETA = 10000.0
NEG = -1e30

STEPS = NT // 2 + 1
EARLY = 24
BANK = SLOT // 2
NSHIFT = 2 * GH


def step_uses(i):
    if i == STEPS - 1:
        return [[(h, NT // 2, 0, BANK), (h + 1, NT // 2, BANK, BANK)] for h in range(0, GH, 2)]
    blocks = [(i, 0, S - P * i)] + ([(NT - i, S - P * i, P * i)] if i else [])
    return [[(h, kb, c, w) for kb, c, w in blocks] for h in range(GH)]


def step_segments(i):
    out = []
    for kb in sorted({kb for blocks in step_uses(i) for _, kb, _, _ in blocks}):
        q = kb * P
        while q < S:
            e = (q // BANK + 1) * BANK
            out.append((kb, q, e))
            q = e
    return out


ALL_STEPS = [(g, i) for g in range(NG) for i in range(STEPS)]
STARTS = [sum(len(step_uses(i)) for _, i in ALL_STEPS[:s]) for s in range(len(ALL_STEPS))]
NS = sum(len(step_uses(i)) for _, i in ALL_STEPS)
assert NS % RING == 0


def max_pieces(g, tiles=range(NT)):
    return [("max", h, t, p) for t in tiles for h in range(g * GH, g * GH + GH)
            for p in range((t * P) // BANK + 1)]


PARTS_OF = {"qkv": 3, "early": 4, "mid": 4, "qT": 2, "kT": 2, "paths": NT}


def in_parts(name):
    return [("part", name, k) for k in range(PARTS_OF.get(name[0], 1) - 1)] + [name]


def between(main, filler):
    out = []
    for n, name in enumerate(main):
        out += [name] + filler[n * len(filler) // len(main):(n + 1) * len(filler) // len(main)]
    return out


def plan_body():
    out = []
    for name in (("early",), ("qkv", 2), ("scores",), ("qkv", 3), ("onehot",)):
        out += in_parts(name)
    for t in range(NJ):
        main = in_parts(("qT", t)) + in_parts(("kT", t)) + in_parts(("mask", t))
        if t < NJ - 1:
            main += in_parts(("mid", t))
        if t + 4 < NT:
            main += in_parts(("qkv", t + 4))
        out += between(main, max_pieces(0, [t - 1]) if t else [])
    main = []
    for t in range(NJ, NT):
        main += in_parts(("qT", t)) + in_parts(("kT", t))
    out += between(main, max_pieces(0, [NJ - 1]))
    main = in_parts(("paths", 0)) + in_parts(("paths", 1))
    second = max_pieces(1)
    out += between(main, max_pieces(0, range(NJ, NT)) + [("shift", 0)] + second[:EARLY])
    rest = second[EARLY:] + [("shift", 1)] + max_pieces(2) + [("shift", 2)] + max_pieces(3) + [("shift", 3)]
    spread = NS - NS // NG - 4
    for s, (g, i) in enumerate(ALL_STEPS):
        uses = step_uses(i)
        segs = [("value", s - 1, k) for k in range(len(step_segments(ALL_STEPS[s - 1][1])))] if s else []
        for k in range(len(uses)):
            n = STARTS[s] + k
            now = [("S", n)]
            if k:
                m = -(-len(segs) // (len(uses) - k))
                now += segs[:m]
                segs = segs[m:]
            if g and i == 2 and k == 0:
                now += [("oT", g - 1)]
            out += between(now, rest[n * len(rest) // spread:(n + 1) * len(rest) // spread]
                           if n < spread else [])
    s = len(ALL_STEPS) - 1
    out += [("value", s, k) for k in range(len(step_segments(ALL_STEPS[s][1])))]
    return out


BODY = plan_body()
HEAD = [("xnT", 0), ("xnT", 1)] + in_parts(("qkv", 0)) + in_parts(("qkv", 1))
TAIL = [("oT", NG - 1), ("attnT", 0), ("attnT", 1), ("proj", 0), ("proj", 1)]
SEAM = ([("xnT", 0), ("xnT", 1), ("oT", NG - 1)] + in_parts(("qkv", 0)) + [("attnT", 0), ("attnT", 1)]
        + in_parts(("qkv", 1)) + [("proj", 0), ("proj", 1)])
assert set(SEAM) == set(HEAD + TAIL)

BY_ACT = {"qkv", "early", "qT", "mask", "shift", "S"}
BY_DVE = {"scores", "kT", "mid", "paths", "max", "oT", "proj"}


def taker(name):
    if name in (("xnT", 0), ("attnT", 0)) or name[0] in BY_ACT:
        return "act"
    if name in (("xnT", 1), ("attnT", 1)) or name[0] in BY_DVE:
        return "dve"
    return None


class Order:

    def __init__(self, names):
        self.names = names
        self.place, self.taken, self.bank, self.before = {}, {}, {}, {}
        self.count = {"act": 0, "dve": 0}
        last = [None] * 6
        big = small = 0
        first_max = next((n for n, x in enumerate(names) if x[0] == "max"), len(names))
        first_seam = len(BODY)
        for n, name in enumerate(names):
            use = name[1] if name[0] == "part" else name
            who = taker(use)
            if who is None:
                continue
            if use not in self.bank:
                if use[0] in ("max", "shift"):
                    self.bank[use] = 4 + small % 2
                    small += 1
                    banks = [self.bank[use]]
                else:
                    width = 2 if first_max < n < first_seam else 3
                    self.bank[use] = 2 * (big % width)
                    big += 1
                    banks = [self.bank[use], self.bank[use] + 1]
                self.before[use] = {last[k] for k in banks}
                for k in banks:
                    last[k] = use
            if name is use:
                self.place[use] = len(self.place) + 1
                self.count[who] += 1
                self.taken[use] = self.count[who]


ORDERS = {"first": Order(HEAD), "loop": Order(BODY + SEAM), "last": Order(BODY + TAIL)}
NU = len(ORDERS["loop"].place)
NTAKEN = ORDERS["loop"].count
SEAM_COUNT = Order(SEAM).count | {"pe": len(Order(SEAM).place)}
TAIL_COUNT = Order(TAIL).count | {"pe": len(TAIL)}
FFN_NORM_AT = 2
FFN_FROM = 4
NORM_AT = NS - NS // NG - 2
FIRST_LINKS, DVE_LINKS = 8, 54


def build(nc, x, wqk, wv, wo, mixk, w1, b1, b1_last, w2, bo1, wo2, bo2, gamma, beta,
          cos_t, sin_t, ident, order, spread, out):
    ctx = ExitStack()
    with ctx:
        def sb(name, shape, dt):
            return ctx.enter_context(nc.sbuf_tensor(name, shape, dt))

        def sem(name):
            return ctx.enter_context(nc.semaphore(name))

        wqk_sb = sb("wqk_sb", [P, NC, 2 * D], F32)
        wv_sb = sb("wv_sb", [P, NC, D], F32)
        wo_sb = sb("wo_sb", [P, NC, D], F32)
        mixk_sb = sb("mixk_sb", [P, NC, 3], F32)
        w1_sb = sb("w1_sb", [P, NC, MID + DM], F32)
        b1_sb = sb("b1_sb", [P, NJ], F32)
        w2_sb = sb("w2_sb", [P, NJ, D], F32)
        wo2_sb = sb("wo2_sb", [P, PATHS], F32)
        bo2_sb = sb("bo2_sb", [P, PATHS], F32)
        gamma_sb = sb("gamma_sb", [P, D], F32)
        beta_sb = sb("beta_sb", [P, D], F32)
        cos_sb = sb("cos_sb", [P, NT, DK], F32)
        sin_sb = sb("sin_sb", [P, NT, DK], F32)
        ident_sb = sb("ident_sb", [P, P], F32)
        ident_bf = sb("ident_bf", [P, P], BF16)
        causal_sb = sb("causal_sb", [P, S], BF16)
        order_sb = sb("order_sb", [P, PATHS], F32)
        xm = sb("xm", [P, NC, S], F32)
        spread_sb = xm[0:PATHS, 0, 0:MID + PATHS]
        spread_bf = sb("spread_bf", [PATHS, MID + PATHS], BF16)
        mhalf = sb("mhalf", [P, NT], F32)
        x_sb = sb("x_sb", [P, NT, D], F32)
        xn = sb("xn", [P, NT, D], F32)
        acc = sb("acc", [P, NT, D], F32)
        xnT = sb("xnT", [P, NC, S + 2], F32)
        attn = xm[:, :, :].rearrange("p c (t d) -> p (c t) d", d=D)
        stats = sb("stats", [P, NT, 6], F32)
        mv = sb("mv", [P, NT, 2], F32)
        ve = sb("ve", [P, NT], F32)
        rs = sb("rs", [P, NT], F32)
        rt = sb("rt", [P, NT], F32)
        rmax = sb("rmax", [P, NT], F32)
        score_sb = sb("score_sb", [P, NT, PATHS], F32)
        req = sb("req", [P, NT, PATHS], F32)
        onehot = sb("onehot", [P, NT, PATHS], BF16)
        onehotT = sb("onehotT", [PATHS, S], BF16)
        mask = sb("mask", [P, 2, S], BF16)
        q_sb = sb("q_sb", [P, 2, 2 * D], F32)
        rope_b = sb("rope_b", [P, 2, 2 * D], F32)
        roped = sb("roped", [P, 2, 2 * D], F32)
        rest = sb("rest", [P, 2 * D], F32)
        v_sb = sb("v_sb", [P, NT, H, VW], F32)
        qT = sb("qT", [PARTS + SHIFT, H, S], BF16)
        kT = sb("kT", [PARTS + SHIFT, H, S], BF16)
        piecemax = sb("piecemax", [P, NT, H, 2], F32)
        rowmax = sb("rowmax", [P, NT, GH], F32)
        shifts = sb("shifts", [P, NT, 2, GH], BF16)
        shiftT = sb("shiftT", [NSHIFT, S], BF16)
        prob = sb("prob", [P, RING, S], F32)
        mid = prob[:, 0:NJ, :]
        hidden = prob[DM:P, NJ - 1, :]
        parts = prob[:, NJ:RING, :].rearrange("p r s -> p (r s)").bitcast(BF16).rearrange(
            "p (i a h n) -> p i a h n", i=2, a=2, h=H)
        attnT = prob[:, 0:NC, :]
        o_sb = sb("o_sb", [P, S], F32)
        rden = sb("rden", [P, NT, GH], F32)
        slots = [ctx.enter_context(nc.psum_tensor(f"slot{i}", [P, SLOT], F32)) for i in range(3)]
        o_ps = ctx.enter_context(nc.psum_tensor("o_ps", [P, SLOT], F32))

        weights_loaded = sem("weights_loaded")
        consts_set = sem("consts_set")
        gates_passed = sem("gates_passed")
        ones_set = sem("ones_set")
        x_loaded = sem("x_loaded")
        slot_filled = sem("slot_filled")
        act_took = sem("act_took")
        dve_took = sem("dve_took")
        dve_linked = sem("dve_linked")
        var_ready = sem("var_ready")
        rsqrt_ready = sem("rsqrt_ready")
        xn_ready = sem("xn_ready")
        acc_begun = sem("acc_begun")
        acc_ffn = sem("acc_ffn")
        mixed = sem("mixed")
        routed = sem("routed")
        onehot_turned = sem("onehot_turned")
        onehot_ready = sem("onehot_ready")
        rope_swapped = sem("rope_swapped")
        rope_done = sem("rope_done")
        hi_cut = sem("hi_cut")
        all_cut = sem("all_cut")
        mid_ready = sem("mid_ready")
        normed = sem("normed")
        shift_cut = sem("shift_cut")
        shift_placed = sem("shift_placed")
        masked = sem("masked")
        pv_done = sem("pv_done")
        o_copied = sem("o_copied")
        out_stored = sem("out_stored")
        NWEIGHTS = 19
        NCONSTS = 8

        def gate(eng):
            eng.sem_inc(gates_passed, 1)

        def now(b, per, k):
            return b * per + k

        def filled(run, b, name):
            o = ORDERS[run].place[name]
            return TAIL_COUNT["pe"] + o if run == "first" else b * NU + SEAM_COUNT["pe"] + o

        def took(run, b, name):
            who = taker(name)
            o = ORDERS[run].taken[name]
            return TAIL_COUNT[who] + o if run == "first" else b * NTAKEN[who] + SEAM_COUNT[who] + o

        def seam_took(b, who):
            return b * NTAKEN[who] + SEAM_COUNT[who]

        def slot_of(run, name):
            k = ORDERS[run].bank[name]
            if name[0] in ("max", "shift"):
                return slots[k // 2][:, k % 2 * BANK:(k % 2 + 1) * BANK]
            return slots[k // 2]

        def every_batch(eng, body):
            with eng.Fori(0, B - 1) as b:
                body("loop", b)
            body("last", B - 1)

        block = ctx.enter_context(nc.Block())

        @block.sync
        def _(sp):
            def load_x(b):
                sp.dma_start(x_sb[:, :, :], x[bass.ds(b, 1)].rearrange("a (t p) d -> p (a t) d", p=P)
                             ).then_inc(x_loaded, 16)

            load_x(0)
            sp.dma_start(ident_sb[:, :], ident).then_inc(weights_loaded, 16)
            sp.dma_start(gamma_sb[:, :], gamma.partition_broadcast(P)).then_inc(weights_loaded, 16)
            sp.dma_start(beta_sb[:, :], beta.partition_broadcast(P)).then_inc(weights_loaded, 16)
            for dst, src in ((mixk_sb, mixk), (wqk_sb, wqk), (wv_sb, wv),
                             (cos_sb, cos_t), (sin_sb, sin_t), (w1_sb, w1), (wo_sb, wo)):
                sp.dma_start(dst[:, :, :], src).then_inc(weights_loaded, 16)
            sp.dma_start(b1_sb[DM:P, NJ - 1:NJ], bo1).then_inc(weights_loaded, 16)
            sp.dma_start(wo2_sb[DM:P, :], wo2).then_inc(weights_loaded, 16)
            sp.dma_start(bo2_sb[:, :], bo2.partition_broadcast(P)).then_inc(weights_loaded, 16)
            sp.dma_start(b1_sb[:, 0:NJ - 1], b1).then_inc(weights_loaded, 16)
            sp.dma_start(b1_sb[0:DM, NJ - 1:NJ], b1_last).then_inc(weights_loaded, 16)
            sp.dma_start(w2_sb[:, 0:NJ - 1, :], w2[0:P * (NJ - 1)].rearrange("(j p) d -> p j d", p=P)
                         ).then_inc(weights_loaded, 16)
            sp.dma_start(w2_sb[0:LAST, NJ - 1, :], w2[P * (NJ - 1):MID + PATHS]).then_inc(weights_loaded, 16)
            sp.dma_start(spread_sb, spread).then_inc(weights_loaded, 16)
            sp.dma_start(order_sb[:, :], order).then_inc(weights_loaded, 16)

            def place_shift(run, b, g):
                sp.wait_ge(act_took, took(run, b, ("shift", g)))
                for k in range(SHIFT):
                    sp.dma_start(qT[PARTS + k:PARTS + k + 1, g * GH:(g + 1) * GH, :],
                                 shiftT[k * GH:(k + 1) * GH, :]).then_inc(shift_placed, 16)

            def store(run, b):
                for i in range(2):
                    sp.wait_ge(dve_took, took(run, b, ("proj", i)))
                    sp.dma_start(out[bass.ds(b, 1), i * S // 2:(i + 1) * S // 2, :]
                                 .rearrange("a (t p) d -> p (a t) d", p=P),
                                 acc[:, i * NT // 2:(i + 1) * NT // 2, :]).then_inc(out_stored, 16)

            def body(run, b):
                if run == "loop":
                    sp.wait_ge(acc_begun, now(b, 1, 1))
                    load_x(b + 1)
                for g in range(NG):
                    place_shift(run, b, g)
                store(run, b)

            every_batch(sp, body)
            sp.wait_ge(out_stored, 32 * B + 32)

        @block.gpsimd
        def _(pool):
            made = [0]

            def make(ins):
                made[0] += 1
                ins.then_inc(consts_set, 1)
                pool.wait_ge(consts_set, made[0])

            make(nc.gpsimd.memset(xnT[:, :, :], 0.0))
            make(nc.gpsimd.memset(v_sb[:, :, :, :], 0.0))
            make(nc.gpsimd.memset(v_sb[:, :, :, DK:DK + 1], 1.0))
            make(nc.gpsimd.memset(mhalf[:, :], -0.5))
            make(nc.gpsimd.memset(causal_sb[:, :], 0.0))
            make(nc.gpsimd.affine_select(out=causal_sb[:, S - P:], in_=causal_sb[:, S - P:],
                                         compare_op=ALU.is_ge, fill=NEG, base=0, pattern=[[-1, P]],
                                         channel_multiplier=1))
            pool.wait_ge(weights_loaded, 16 * NWEIGHTS)
            make(nc.gpsimd.tensor_copy(ident_bf[:, :], ident_sb[:, :]))
            make(nc.gpsimd.tensor_copy(spread_bf[:, :], spread_sb))
            assert made[0] == NCONSTS
            pool.sem_inc(out_stored, 32)

            def rsqrt(value):
                pool.wait_ge(var_ready, value)
                nc.gpsimd.tensor_tensor(rs[:, :], ve[:, :], mhalf[:, :], ALU.pow).then_inc(rsqrt_ready, 1)

            def swap(run, b, t):
                if t < 2:
                    pool.wait_ge(act_took, seam_took(b, "act"))
                else:
                    pool.wait_ge(act_took, took(run, b, ("qkv", t)))
                    pool.wait_ge(rope_done, now(b, NT, t - 1))
                q4 = q_sb[:, t % 2, :].rearrange("p (h d) -> p h d", d=DK)
                r4 = rope_b[:, t % 2, :].rearrange("p (h d) -> p h d", d=DK)
                hd = DK // 2
                for a, z in ((0, hd), (hd, 0)):
                    ins = nc.gpsimd.tensor_tensor(
                        r4[:, :, a:a + hd], q4[:, :, z:z + hd],
                        sin_sb[:, t, None, a:a + hd].to_broadcast([P, 2 * H, hd]), ALU.mult)
                ins.then_inc(rope_swapped, 1)

            def add_ffn(b, k):
                t = k // 2
                if k % 2 == 0:
                    pool.wait_ge(normed, now(b, NT, t + 1))
                    nc.gpsimd.tensor_tensor(xn[:, t, :], xn[:, t, :], gamma_sb[:, :],
                                            ALU.mult).then_inc(acc_ffn, 1)
                else:
                    pool.wait_ge(acc_ffn, now(b, 2 * NT, k))
                    nc.gpsimd.tensor_tensor(acc[:, t, :], acc[:, t, :], xn[:, t, :],
                                            ALU.add).then_inc(acc_ffn, 1)

            def mask_diagonal(run, b, s, k):
                n = STARTS[s] + k
                pool.wait_ge(act_took, took(run, b, ("S", n)))
                gate(pool)
                for _, _, c, _ in step_uses(ALL_STEPS[s][1])[k]:
                    d = prob[:, n % RING, c:c + P]
                    ins = nc.gpsimd.affine_select(out=d, in_=d, compare_op=ALU.is_ge, fill=0.0, base=0,
                                                  pattern=[[1, P]], channel_multiplier=-1)
                ins.then_inc(masked, 1)

            def body(run, b):
                for t in range(NT):
                    swap(run, b, t)
                    if t == NT // 2:
                        pool.wait_ge(out_stored, now(b, 32, 32))
                        nc.gpsimd.tensor_tensor(acc[:, :, :], x_sb[:, :, :],
                                                beta_sb[:, None, :].to_broadcast([P, NT, D]),
                                                ALU.add).then_inc(acc_begun, 1)
                rsqrt(now(b, 2, 2))
                for s, (_, i) in enumerate(ALL_STEPS):
                    for k in range(len(step_uses(i))):
                        mask_diagonal(run, b, s, k)
                        n = STARTS[s] + k
                        if FFN_FROM <= n < FFN_FROM + 2 * NT:
                            add_ffn(b, n - FFN_FROM)
                        if run == "loop" and n == NORM_AT:
                            rsqrt(now(b, 2, 3))

            rsqrt(1)
            every_batch(pool, body)

        @block.scalar
        def _(act):
            act.sem_inc(act_took, TAIL_COUNT["act"])
            act.wait_ge(weights_loaded, 16 * NWEIGHTS)
            act.wait_ge(consts_set, NCONSTS)

            def take(run, b, name):
                act.wait_ge(slot_filled, filled(run, b, name))
                return slot_of(run, name)

            def copy_turned(run, b, name):
                ps = take(run, b, name)
                dst = xnT[:, 0, 1:S + 1] if name[0] == "xnT" else attnT[:, 0, :]
                nc.scalar.copy(dst, ps[:, :]).then_inc(act_took, 1)

            def copy_qkv(run, b, t):
                if t >= 2:
                    act.wait_ge(rope_done, now(b, NT, t - 1))
                ps = take(run, b, ("qkv", t))
                nc.scalar.copy(q_sb[:, t % 2, :], ps[:, 0:2 * D])
                nc.scalar.copy(v_sb[:, t, :, 0:DK],
                               ps[:, 2 * D:3 * D].rearrange("p (h d) -> p h d", d=DK)
                               ).then_inc(act_took, 1)

            def cut_hi(run, b, t):
                act.wait_ge(rope_done, now(b, NT, t + 1))
                if t >= 2:
                    act.wait_ge(slot_filled, filled(run, b, ("kT", t - 2)))
                pt = parts[:, t % 2, :, :, :].rearrange("p a h (n d) -> p a h n d", d=DK)
                r = roped[:, t % 2, :].rearrange("p (a h d) -> p a h d", a=2, d=DK)
                nc.scalar.copy(pt[:, 0, :, 0:6:3, :], r[:, 0, :, None, :].to_broadcast([P, H, 2, DK]))
                nc.scalar.copy(pt[:, 0, :, 5, :], r[:, 0, :, :])
                nc.scalar.copy(pt[:, 1, :, 0:3, :], r[:, 1, :, None, :].to_broadcast([P, H, 3, DK])
                               ).then_inc(hi_cut, 1)

            def copy_qT(run, b, t):
                ps = take(run, b, ("qT", t))
                nc.scalar.copy(qT[0:PARTS, :, t * P:(t + 1) * P],
                               ps[0:PARTS, :].bitcast(BF16).rearrange("p (h c) -> p h c", c=P)
                               ).then_inc(act_took, 1)

            def activate_early(run, b):
                ps = take(run, b, ("early",))
                nc.scalar.activation(hidden, ps[DM:P, :], ACT.Tanh, bias=b1_sb[DM:P, NJ - 1:NJ])
                nc.scalar.activation(mid[0:DM, NJ - 1, :], ps[0:DM, :], ACT.Identity,
                                     bias=b1_sb[0:DM, NJ - 1:NJ]).then_inc(act_took, 1)

            def copy_mask(run, b, j):
                if j >= 2:
                    act.wait_ge(dve_took, took(run, b, ("mid", j - 2)))
                ps = take(run, b, ("mask", j))
                rows = P if j < NJ - 1 else LAST
                nc.scalar.copy(mask[0:rows, j % 2, :], ps[0:rows, :]).then_inc(act_took, 1)

            def copy_shift(run, b, g):
                if g:
                    act.wait_ge(shift_placed, now(b, 32 * NG, 32 * g))
                ps = take(run, b, ("shift", g))
                nc.scalar.copy(shiftT[:, :], ps[0:NSHIFT, :].bitcast(BF16)).then_inc(act_took, 1)

            def exponentiate(run, b, n):
                if n >= RING:
                    act.wait_ge(pv_done, now(b, len(ALL_STEPS), step_of(n - RING) + 1))
                ps = take(run, b, ("S", n))
                nc.scalar.activation(prob[:, n % RING, :], ps[:, :], ACT.Exp,
                                     scale=float(DK) ** -0.5).then_inc(act_took, 1)

            def walk(run, b, names):
                for name in names:
                    what = name[0]
                    if what == "qkv":
                        copy_qkv(run, b, name[1])
                        if name[1] == 2:
                            cut_hi(run, b, 1)
                    elif name in (("xnT", 0), ("attnT", 0)):
                        copy_turned(run, b, name)
                    elif what == "early":
                        activate_early(run, b)
                        cut_hi(run, b, 0)
                    elif what == "qT":
                        copy_qT(run, b, name[1])
                        if name[1] == NJ:
                            cut_hi(run, b, NT - 1)
                    elif what == "mask":
                        copy_mask(run, b, name[1])
                        cut_hi(run, b, name[1] + 2)
                    elif what == "shift":
                        copy_shift(run, b, name[1])
                    elif what == "S":
                        exponentiate(run, b, name[1])

            walk("first", 0, HEAD)
            every_batch(act, lambda run, b: walk(run, b, ORDERS[run].names))

        @block.vector
        def _(dve):
            dve.sem_inc(dve_took, TAIL_COUNT["dve"])
            nc.vector.memset(kT[PARTS:PARTS + SHIFT, :, :], 1.0).then_inc(ones_set, 1)
            nc.vector.memset(piecemax[:, :, :, :], NEG).then_inc(ones_set, 1)
            dve.wait_ge(ones_set, 2)
            links = {"first": 0, "loop": 0, "last": 0}

            def link(run, b, ins):
                links[run] += 1
                ins.then_inc(dve_linked, 1)
                dve.wait_ge(dve_linked, links[run] if run == "first" else
                            FIRST_LINKS + now(b, DVE_LINKS, links[run]))

            def take(run, b, name):
                dve.wait_ge(slot_filled, filled(run, b, name))
                return slot_of(run, name)

            def norm_stats(run, b, src):
                for t in range(NT):
                    ins = nc.vector.bn_stats(stats[:, t, :], src[:, t, :])
                link(run, b, ins)
                gate(dve)
                for t in range(NT):
                    ins = nc.vector.bn_aggr(mv[:, t, :], stats[:, t, :])
                link(run, b, ins)
                nc.vector.tensor_scalar(ve[:, :], mv[:, :, 1], EPS, None, ALU.add).then_inc(var_ready, 1)

            def norm_root(run, b, value):
                dve.wait_ge(rsqrt_ready, value)
                link(run, b, nc.vector.tensor_tensor(rt[:, :], rs[:, :], rs[:, :], ALU.mult))
                link(run, b, nc.vector.tensor_tensor(rt[:, :], rt[:, :], ve[:, :], ALU.mult))
                link(run, b, nc.vector.tensor_scalar(rt[:, :], rt[:, :], -0.5, 1.5, ALU.mult, ALU.add))
                link(run, b, nc.vector.tensor_tensor(rt[:, :], rs[:, :], rt[:, :], ALU.mult))

            def normalize(dst, src, signal):
                for t in range(NT):
                    nc.vector.tensor_scalar(dst[:, t, :], src[:, t, :], mv[:, t, 0:1], rt[:, t:t + 1],
                                            ALU.subtract, ALU.mult).then_inc(signal, 1)

            def copy_turned(run, b, name):
                ps = take(run, b, name)
                dst = xnT[:, 1, 1:S + 1] if name[0] == "xnT" else attnT[:, 1, :]
                nc.vector.tensor_copy(dst, ps[:, :]).then_inc(dve_took, 1)

            def mix(run, b):
                dve.wait_ge(act_took, took(run, b, ("xnT", 0)))
                dve.wait_ge(dve_took, took(run, b, ("xnT", 1)))
                for k in range(3):
                    for c in range(NC):
                        if k == 0:
                            ins = nc.vector.tensor_scalar(xm[:, c, :], xnT[:, c, 0:S], mixk_sb[:, c, 0:1],
                                                          None, ALU.mult)
                        else:
                            ins = nc.vector.scalar_tensor_tensor(xm[:, c, :], xnT[:, c, k:k + S],
                                                                 mixk_sb[:, c, k:k + 1], xm[:, c, :],
                                                                 ALU.mult, ALU.add)
                    if k < 2:
                        link(run, b, ins)
                ins.then_inc(mixed, 1)

            def rotate(run, b, t):
                dve.wait_ge(act_took, seam_took(b, "act") if t < 2 else took(run, b, ("qkv", t)))
                if t >= 2:
                    dve.wait_ge(hi_cut, now(b, NT, t - 1))
                link(run, b, nc.vector.tensor_tensor(
                    roped[:, t % 2, :].rearrange("p (h d) -> p h d", d=DK),
                    q_sb[:, t % 2, :].rearrange("p (h d) -> p h d", d=DK),
                    cos_sb[:, t, None, :].to_broadcast([P, 2 * H, DK]), ALU.mult))
                dve.wait_ge(rope_swapped, now(b, NT, t + 1))
                nc.vector.tensor_tensor(roped[:, t % 2, :], roped[:, t % 2, :], rope_b[:, t % 2, :],
                                        ALU.add).then_inc(rope_done, 1)

            def cut_rest(run, b, t):
                dve.wait_ge(hi_cut, now(b, NT, t + 1))
                pt = parts[:, t % 2, :, :, :].rearrange("p a h (n d) -> p a h n d", d=DK)
                r = roped[:, t % 2, :].rearrange("p (a h d) -> p a h d", a=2, d=DK)
                e = rest[:, :].rearrange("p (a h d) -> p a h d", a=2, d=DK)
                link(run, b, nc.vector.tensor_tensor(e, r, pt[:, :, :, 0, :], ALU.subtract))
                nc.vector.tensor_copy(pt[:, 0, :, 1:5:3, :], e[:, 0, :, None, :].to_broadcast([P, H, 2, DK]))
                link(run, b, nc.vector.tensor_copy(pt[:, 1, :, 3:5, :],
                                                   e[:, 1, :, None, :].to_broadcast([P, H, 2, DK])))
                nc.vector.tensor_tensor(pt[:, 0, :, 2, :], e[:, 0], pt[:, 0, :, 1, :], ALU.subtract)
                nc.vector.tensor_tensor(pt[:, 1, :, 5, :], e[:, 1], pt[:, 1, :, 3, :],
                                        ALU.subtract).then_inc(all_cut, 1)

            def copy_kT(run, b, t):
                ps = take(run, b, ("kT", t))
                nc.vector.tensor_copy(kT[0:PARTS, :, t * P:(t + 1) * P],
                                      ps[0:PARTS, :].bitcast(BF16).rearrange("p (h c) -> p h c", c=P)
                                      ).then_inc(dve_took, 1)

            def route(run, b):
                ps = take(run, b, ("scores",))
                tiles = [P, NT, PATHS]
                nc.vector.tensor_tensor(score_sb[:, :, :],
                                        ps[:, 0:NT * PATHS].rearrange("p (t n) -> p t n", n=PATHS),
                                        bo2_sb[:, None, :].to_broadcast(tiles), ALU.add).then_inc(dve_took, 1)
                dve.wait_ge(dve_took, took(run, b, ("scores",)))
                link(run, b, nc.vector.tensor_reduce(rmax[:, :], score_sb[:, :, :], AX.X, ALU.max))
                top = rmax[:, :, None].to_broadcast(tiles)
                link(run, b, nc.vector.tensor_tensor(req[:, :, :], score_sb[:, :, :], top, ALU.is_equal))
                link(run, b, nc.vector.tensor_tensor(req[:, :, :], req[:, :, :],
                                                     order_sb[:, None, :].to_broadcast(tiles), ALU.mult))
                link(run, b, nc.vector.tensor_reduce(rmax[:, :], req[:, :, :], AX.X, ALU.max))
                nc.vector.tensor_tensor(onehot[:, :, :], req[:, :, :], top, ALU.is_equal).then_inc(routed, 1)

            def copy_onehotT(b):
                dve.wait_ge(onehot_turned, now(b, 1, 1))
                nc.vector.tensor_copy(onehotT[:, :], o_ps[0:PATHS, 0:BANK].bitcast(BF16)
                                      ).then_inc(onehot_ready, 1)

            def select_mid(run, b, j):
                dve.wait_ge(act_took, took(run, b, ("mask", j)))
                ps = take(run, b, ("mid", j))
                nc.vector.scalar_tensor_tensor(mid[:, j, :], ps[:, :], b1_sb[:, j:j + 1], mask[:, j % 2, :],
                                               ALU.add, ALU.mult).then_inc(dve_took, 1)

            def select_last(run, b):
                dve.wait_ge(act_took, took(run, b, ("mask", NJ - 1)))
                m = mask[:, (NJ - 1) % 2, :]
                nc.vector.tensor_copy(mid[DM:LAST, NJ - 1, :], m[DM:LAST, :])
                nc.vector.tensor_tensor(mid[0:DM, NJ - 1, :], mid[0:DM, NJ - 1, :], m[0:DM, :],
                                        ALU.mult).then_inc(mid_ready, 1)

            def add_paths(run, b, i):
                ps = take(run, b, ("paths", i))
                y = xn[:, i * NT // 2:(i + 1) * NT // 2, :]
                nc.vector.tensor_tensor(y, ps[:, :].rearrange("p (t d) -> p t d", d=D), y,
                                        ALU.add).then_inc(dve_took, 1)
                if i:
                    dve.wait_ge(dve_took, took(run, b, ("paths", 1)))
                    norm_stats(run, b, xn)

            def max_piece(run, b, h, t, p):
                ps = take(run, b, ("max", h, t, p))
                gate(dve)
                end = (t + 1) * P
                w = min(BANK, end - p * BANK)
                at = S - end + p * BANK
                nc.vector.tensor_tensor_reduce(ps[:, 0:w], ps[:, 0:w], causal_sb[:, at:at + w],
                                               1.0, NEG, ALU.add, ALU.max,
                                               piecemax[:, t, h, p:p + 1]).then_inc(dve_took, 1)

            def cut_shift(run, b, g):
                dve.wait_ge(dve_took, took(run, b, max_pieces(g)[-1]))
                link(run, b, nc.vector.tensor_reduce(rowmax[:, :, :], piecemax[:, :, g * GH:(g + 1) * GH, :],
                                                     AX.X, ALU.max))
                link(run, b, nc.vector.tensor_scalar(shifts[:, :, 0, :], rowmax[:, :, :], -1.0, None, ALU.mult))
                nc.vector.scalar_tensor_tensor(shifts[:, :, 1, :], rowmax[:, :, :], -1.0, shifts[:, :, 0, :],
                                               ALU.mult, ALU.subtract).then_inc(shift_cut, 1)

            def copy_sums(run, b, g):
                dve.wait_ge(pv_done, now(b, len(ALL_STEPS), STEPS * (g + 1)))
                if g:
                    dve.wait_ge(slot_filled, filled(run, b, ("oT", g - 1)))
                nc.vector.tensor_copy(o_sb[:, :], o_ps[:, :]).then_inc(o_copied, 1)

            def divide_sums(run, b, g):
                ps = take(run, b, ("oT", g))
                o4 = ps[:, :].rearrange("p (t h v) -> p t h v", h=GH, v=VW)
                link(run, b, nc.vector.reciprocal(rden[:, :, :], o4[:, :, :, DK]))
                nc.vector.tensor_tensor(
                    attn[:, :, g * GH * DK:(g + 1) * GH * DK].rearrange("p t (h d) -> p t h d", d=DK),
                    o4[:, :, :, 0:DK], rden[:, :, :, None].to_broadcast([P, NT, GH, DK]),
                    ALU.mult).then_inc(dve_took, 1)

            def finish(run, b, i):
                if i == 0:
                    dve.wait_ge(acc_ffn, now(b, 2 * NT, 2 * NT))
                ps = take(run, b, ("proj", i))
                a = acc[:, i * NT // 2:(i + 1) * NT // 2, :]
                nc.vector.tensor_tensor(a, ps[:, :].rearrange("p (t d) -> p t d", d=D), a,
                                        ALU.add).then_inc(dve_took, 1)

            def walk(run, b, names):
                for name in names:
                    what = name[0]
                    if name in (("xnT", 1), ("attnT", 1)):
                        copy_turned(run, b, name)
                        if what == "attnT" and run == "loop":
                            mix(run, b)
                    elif what == "early":
                        rotate(run, b, 0)
                        rotate(run, b, 1)
                        cut_rest(run, b, 0)
                    elif what == "scores":
                        route(run, b)
                        rotate(run, b, 2)
                        cut_rest(run, b, 1)
                    elif what == "onehot":
                        copy_onehotT(b)
                    elif what == "kT":
                        copy_kT(run, b, name[1])
                        if name[1] + 3 < NT:
                            rotate(run, b, name[1] + 3)
                        if name[1] == NJ:
                            cut_rest(run, b, NT - 1)
                    elif what == "mid":
                        select_mid(run, b, name[1])
                        cut_rest(run, b, name[1] + 2)
                    elif what == "mask" and name[1] == NJ - 1:
                        select_last(run, b)
                        cut_rest(run, b, name[1] + 2)
                    elif what == "paths":
                        add_paths(run, b, name[1])
                    elif what == "max":
                        max_piece(run, b, *name[1:])
                    elif what == "shift":
                        cut_shift(run, b, name[1])
                    elif what == "S" and name[1] == FFN_NORM_AT:
                        norm_root(run, b, now(b, 2, 2))
                        normalize(xn, xn, normed)
                    elif what == "S" and run == "loop" and name[1] == NORM_AT:
                        dve.wait_ge(x_loaded, 16 * (b + 2))
                        norm_stats(run, b, x_sb)
                        dve.wait_ge(acc_ffn, now(b, 2 * NT, 2 * NT))
                        norm_root(run, b, now(b, 2, 3))
                        normalize(xn, x_sb, xn_ready)
                    elif what == "value":
                        g, i = ALL_STEPS[name[1]]
                        if i == STEPS - 1 and name[2] == len(step_segments(i)) - 1:
                            copy_sums(run, b, g)
                    elif what == "oT":
                        divide_sums(run, b, name[1])
                    elif what == "proj":
                        finish(run, b, name[1])

            dve.wait_ge(weights_loaded, 16 * NWEIGHTS)
            dve.wait_ge(consts_set, NCONSTS)
            dve.wait_ge(x_loaded, 16)
            norm_stats("first", 0, x_sb)
            norm_root("first", 0, 1)
            normalize(xn, x_sb, xn_ready)
            walk("first", 0, HEAD)
            mix("first", 0)
            assert links["first"] == FIRST_LINKS, links
            every_batch(dve, lambda run, b: walk(run, b, ORDERS[run].names))
            assert links["loop"] == DVE_LINKS, links

        @block.tensor
        def _(pe):
            pe.wait_ge(weights_loaded, 16 * NWEIGHTS)
            pe.wait_ge(consts_set, NCONSTS)
            pe.wait_ge(ones_set, 2)
            pe.sem_inc(slot_filled, TAIL_COUNT["pe"])

            def begin(run, b, name):
                need = {}
                for old in ORDERS[run].before[name] - {None}:
                    who = taker(old)
                    need[who] = max(need.get(who, 0), ORDERS[run].taken[old])
                for who, o in need.items():
                    base = TAIL_COUNT[who] if run == "first" else b * NTAKEN[who] + SEAM_COUNT[who]
                    pe.wait_ge(act_took if who == "act" else dve_took, base + o)
                return slot_of(run, name)

            def turn(run, b, name):
                what, c = name
                if name == ("xnT", 0):
                    pe.wait_ge(xn_ready, NT if run == "first" else now(b + 1, NT, NT))
                if name == ("attnT", 0):
                    pe.wait_ge(dve_took, took(run, b, ("oT", NG - 1)))
                if what == "oT":
                    pe.wait_ge(o_copied, now(b, NG, c + 1))
                ps = begin(run, b, name)
                for t in range(NT):
                    if what == "oT":
                        src = o_sb[:, t * P:(t + 1) * P]
                    else:
                        src = (xn if what == "xnT" else attn)[:, t, c * P:(c + 1) * P]
                    ins = nc.tensor.transpose(ps[:, t * P:(t + 1) * P], src, ident_sb[:, :])
                ins.then_inc(slot_filled, 1)

            def project(run, b, name, k):
                ps = begin(run, b, name) if k == 0 else slot_of(run, name)
                t = name[1]
                if t == 0 and k == 0:
                    pe.wait_ge(act_took, took(run, b, ("xnT", 0)))
                    pe.wait_ge(dve_took, took(run, b, ("xnT", 1)))
                todo = [(wqk_sb, 0, 2 * D, c) for c in range(NC)], [(wv_sb, 2 * D, D, c) for c in range(NC)]
                for w, a, n, c in (todo[0][:1], todo[0][1:], todo[1])[k]:
                    ins = nc.tensor.matmul(ps[:, a:a + n], xnT[:, c, 1 + t * P:1 + (t + 1) * P], w[:, c, :],
                                           start=(c == 0), stop=(c == NC - 1))
                return ins

            def middle(run, b, name, k):
                ps = begin(run, b, name) if k == 0 else slot_of(run, name)
                j = NJ - 1 if name[0] == "early" else name[1]
                if name[0] == "early" and k == 0:
                    pe.wait_ge(mixed, now(b, 1, 1))
                n, c = k // NC * BANK, k % NC
                return nc.tensor.matmul(ps[:, n:n + BANK], w1_sb[:, c, j * P:(j + 1) * P],
                                        xm[:, c, n:n + BANK], start=(c == 0), stop=(c == NC - 1))

            def router_scores(run, b):
                ps = begin(run, b, ("scores",))
                pe.wait_ge(act_took, took(run, b, ("early",)))
                for t in range(NT):
                    ins = nc.tensor.matmul(ps[:, t * PATHS:(t + 1) * PATHS], hidden[:, t * P:(t + 1) * P],
                                           wo2_sb[DM:P, :], start=True, stop=True)
                ins.then_inc(slot_filled, 1)

            def turn_onehot(b):
                pe.wait_ge(routed, now(b, 1, 1))
                view = o_ps[0:PATHS, 0:BANK].bitcast(BF16)
                for t in range(NT):
                    ins = nc.tensor.transpose(view[:, t * P:(t + 1) * P], onehot[:, t, :], ident_bf[:, :])
                ins.then_inc(onehot_turned, 1)

            def spread_mask(run, b, j):
                ps = begin(run, b, ("mask", j))
                if j == 0:
                    pe.wait_ge(onehot_ready, now(b, 1, 1))
                rows = P if j < NJ - 1 else LAST
                for n in range(0, S, BANK):
                    ins = nc.tensor.matmul(ps[0:rows, n:n + BANK], spread_bf[:, j * P:j * P + rows],
                                           onehotT[:, n:n + BANK], start=True, stop=True)
                ins.then_inc(slot_filled, 1)

            def turn_parts(run, b, name, k):
                what, t = name
                ps = begin(run, b, name) if k == 0 else slot_of(run, name)
                if what == "qT" and k == 0:
                    pe.wait_ge(all_cut, now(b, NT, t + 1))
                view = ps[0:PARTS, :].bitcast(BF16)
                for h in range(k * H // 2, (k + 1) * H // 2):
                    ins = nc.tensor.transpose(view[:, h * P:(h + 1) * P],
                                              parts[:, t % 2, 0 if what == "qT" else 1, h, :], ident_bf[:, :])
                return ins

            def paths_out(run, b, name, k):
                ps = begin(run, b, name) if k == 0 else slot_of(run, name)
                if name[1] == 0 and k == 0:
                    pe.wait_ge(dve_took, took(run, b, ("mid", NJ - 2)))
                    pe.wait_ge(mid_ready, now(b, 1, 1))
                m = k // 2
                t = name[1] * NT // 2 + m
                for j in (range(3), range(3, NJ))[k % 2]:
                    rows = P if j < NJ - 1 else LAST
                    ins = nc.tensor.matmul(ps[:, m * D:(m + 1) * D], mid[0:rows, j, t * P:(t + 1) * P],
                                           w2_sb[0:rows, j, :], start=(j == 0), stop=(j == NJ - 1))
                return ins

            def max_scores(run, b, h, t, p):
                if h % GH == 0 and p == 0 and h == 0:
                    pe.wait_ge(act_took, took(run, b, ("qT", t)))
                    pe.wait_ge(dve_took, took(run, b, ("kT", t)))
                ps = begin(run, b, ("max", h, t, p))
                w = min(BANK, (t + 1) * P - p * BANK)
                nc.tensor.matmul(ps[:, 0:w], qT[0:PARTS, h, t * P:(t + 1) * P],
                                 kT[0:PARTS, h, p * BANK:p * BANK + w],
                                 start=True, stop=True).then_inc(slot_filled, 1)

            def turn_shift(run, b, g):
                pe.wait_ge(shift_cut, now(b, NG, g + 1))
                ps = begin(run, b, ("shift", g))
                view = ps[0:NSHIFT, :].bitcast(BF16)
                for t in range(NT):
                    ins = nc.tensor.transpose(view[:, t * P:(t + 1) * P],
                                              shifts[:, t, :, :].rearrange("p a h -> p (a h)"), ident_bf[:, :])
                ins.then_inc(slot_filled, 1)

            def score(run, b, s, k):
                g, i = ALL_STEPS[s]
                if i == 0 and k == 0:
                    pe.wait_ge(shift_placed, now(b, 32 * NG, 32 * (g + 1)))
                ps = begin(run, b, ("S", STARTS[s] + k))
                for hh, kb, c0, w in step_uses(i)[k]:
                    h = g * GH + hh
                    c = c0
                    while c < c0 + w:
                        e = min(c0 + w, (c // BANK + 1) * BANK)
                        q = kb * P + c - c0
                        ins = nc.tensor.matmul(ps[:, c:e], kT[:, h, kb * P:(kb + 1) * P],
                                               qT[:, h, q:q + e - c], start=True, stop=True)
                        c = e
                ins.then_inc(slot_filled, 1)

            def values(run, b, s, k):
                g, i = ALL_STEPS[s]
                uses, segments = step_uses(i), step_segments(i)
                if k == 0:
                    pe.wait_ge(masked, now(b, NS, STARTS[s] + len(uses)))
                    if g and i == 0:
                        pe.wait_ge(o_copied, now(b, NG, g))
                kb, q, e = segments[k]
                where = {hh: (n, c0) for n, blocks in enumerate(uses) for hh, kk, c0, _ in blocks if kk == kb}
                for hh in range(GH):
                    n, c0 = where[hh]
                    c = c0 + q - kb * P
                    ins = nc.tensor.matmul(o_ps[VW * hh:VW * (hh + 1), q:e], v_sb[:, kb, g * GH + hh, :],
                                           prob[:, (STARTS[s] + n) % RING, c:c + e - q],
                                           start=(kb == 0), stop=(kb == (NT // 2 if q >= BANK else NT // 2 - 1)))
                if k == len(segments) - 1:
                    ins.then_inc(pv_done, 1)

            def out_project(run, b, i):
                ps = begin(run, b, ("proj", i))
                if i == 0:
                    pe.wait_ge(act_took, took(run, b, ("attnT", 0)))
                    pe.wait_ge(dve_took, took(run, b, ("attnT", 1)))
                for k in range(NT // 2):
                    t = i * NT // 2 + k
                    for c in range(NC):
                        ins = nc.tensor.matmul(ps[:, k * D:(k + 1) * D], attnT[:, c, t * P:(t + 1) * P],
                                               wo_sb[:, c, :], start=(c == 0), stop=(c == NC - 1))
                ins.then_inc(slot_filled, 1)

            def walk(run, b, names):
                if run != "first":
                    pe.wait_ge(act_took, seam_took(b, "act"))
                    pe.wait_ge(dve_took, seam_took(b, "dve"))
                for name in names:
                    what = name[0]
                    use, k = name[1:] if what == "part" else (name, PARTS_OF.get(what, 1) - 1)
                    if use[0] in PARTS_OF:
                        write = {"qkv": project, "early": middle, "mid": middle, "qT": turn_parts,
                                 "kT": turn_parts, "paths": paths_out}[use[0]]
                        ins = write(run, b, use, k)
                        if what != "part":
                            ins.then_inc(slot_filled, 1)
                    elif what in ("xnT", "oT", "attnT"):
                        turn(run, b, name)
                    elif what == "scores":
                        router_scores(run, b)
                    elif what == "onehot":
                        turn_onehot(b)
                    elif what == "mask":
                        spread_mask(run, b, name[1])
                    elif what == "max":
                        max_scores(run, b, *name[1:])
                    elif what == "shift":
                        turn_shift(run, b, name[1])
                    elif what == "S":
                        s = step_of(name[1])
                        score(run, b, s, name[1] - STARTS[s])
                    elif what == "value":
                        values(run, b, *name[1:])
                    elif what == "proj":
                        out_project(run, b, name[1])

            walk("first", 0, HEAD)
            every_batch(pe, lambda run, b: walk(run, b, ORDERS[run].names))


def step_of(n):
    return max(s for s in range(len(ALL_STEPS)) if STARTS[s] <= n)


def kernel(**inputs):
    import numpy as _np
    import concourse.bacc as _bacc
    from concourse import mybir as _mybir
    from concourse.bass_utils import run_bass_kernel_spmd as _run

    a = {k: _np.asarray(v) for k, v in inputs.items()}

    def chunks(w):
        return w.reshape(w.shape[0] // P, P, w.shape[1]).transpose(1, 0, 2)

    pair = _np.concatenate([_np.arange(0, DK, 2), _np.arange(1, DK, 2)])
    rows = (_np.arange(H)[:, None] * DK + pair[None, :]).reshape(-1)
    wqk = _np.concatenate([a["L0_attn_Wq"][rows], a["L0_attn_Wk"][rows]], axis=0).T
    w2 = _np.concatenate([a["L0_ffn_W2"].reshape(MID, D), a["L0_ffn_b2"]], axis=0)

    rates = _np.float32(THETA) ** (-(_np.float32(2.0) * _np.arange(DK // 2, dtype=_np.float32)) / _np.float32(DK))
    angle = _np.arange(S, dtype=_np.float32)[:, None] * rates[None, :].astype(_np.float32)
    cos, sin = _np.cos(angle), _np.sin(angle)
    cos_t = _np.concatenate([cos, cos], axis=1).astype(_np.float32)
    sin_t = _np.concatenate([-sin, sin], axis=1).astype(_np.float32)

    spread = _np.concatenate([_np.repeat(_np.eye(PATHS), DM, axis=1), _np.eye(PATHS)], axis=1)

    sent = {
        "x": a["L0_attn_x"],
        "wqk": chunks(wqk),
        "wv": chunks(a["L0_attn_Wv"].T),
        "wo": chunks(a["L0_attn_Wo"].T),
        "mixk": chunks(a["L0_ffn_mix_kernel"].T),
        "w1": chunks(_np.concatenate([a["L0_ffn_W1"].transpose(1, 0, 2).reshape(D, MID),
                                      a["L0_ffn_Wo1"]], axis=1)),
        "b1": a["L0_ffn_b1"].reshape(MID)[:P * (NJ - 1)].reshape(NJ - 1, P).T,
        "b1_last": a["L0_ffn_b1"][PATHS - 1].reshape(DM, 1),
        "w2": w2,
        "bo1": a["L0_ffn_bo1"].reshape(DM, 1),
        "wo2": a["L0_ffn_Wo2"],
        "bo2": a["L0_ffn_bo2"],
        "gamma": a["L0_ffn_gamma"],
        "beta": a["L0_ffn_beta"],
        "cos_t": chunks(cos_t),
        "sin_t": chunks(sin_t),
        "ident": _np.eye(P, dtype=_np.float32),
        "spread": spread.astype(_np.float32),
        "order": _np.tile(_np.arange(PATHS, 0, -1, dtype=_np.float32), (P, 1)),
    }
    nc = _bacc.Bacc("TRN2", target_bir_lowering=False, num_devices=1)
    arrays, args = {}, {}
    for name, v in sent.items():
        v = _np.ascontiguousarray(v)
        arrays[f"in_{name}"] = v
        args[name] = nc.dram_tensor(f"in_{name}", v.shape, _mybir.dt.from_np(v.dtype), kind="ExternalInput").ap()
    args["out"] = nc.dram_tensor("out_0", (B, S, D), F32, kind="ExternalOutput").ap()
    build(nc, **args)
    r = _run(nc, [arrays], core_ids=[0])
    return r.results[0]["out_0"]
```

```python
from contextlib import ExitStack

import concourse.bass as bass
from concourse import mybir

ALU = mybir.AluOpType
ACT = mybir.ActivationFunctionType
AX = mybir.AxisListType
BF16 = mybir.dt.bfloat16
F32 = mybir.dt.float32

B, S, D = 4, 1024, 256
H = 16
DK = D // H
P = 128
NT = S // P
NC = D // P
PATHS = 9
DM = D // 4
MID = PATHS * DM
NJ = (MID + P - 1) // P
LAST_ROWS = DM + PATHS
PARTS = 6 * DK
SHIFT = 2
VW = 32
GH = 4
NG = H // GH
RING = 8
SLOT = 1024
EPS = 1e-5
THETA = 10000.0
NEG = -1e30

STEPS = NT // 2 + 1
MAXIMA_END = 51
ALONG = 4
EARLY = 8
ALONG_LAST = 0
BESIDE_TILE = 8
BANK = SLOT // 2
CUT_LAG = 3
FILLER_COST = 64
NSHIFT = 2 * GH


def step_uses(i):
    if i == STEPS - 1:
        return [[(h, NT // 2, 0, BANK), (h + 1, NT // 2, BANK, BANK)] for h in range(0, GH, 2)]
    blocks = [(i, 0, S - P * i)] + ([(NT - i, S - P * i, P * i)] if i else [])
    return [[(h, kb, c, w) for kb, c, w in blocks] for h in range(GH)]


def step_segments(i):
    out = []
    for kb in sorted({kb for blocks in step_uses(i) for _, kb, _, _ in blocks}):
        q = kb * P
        while q < S:
            e = (q // BANK + 1) * BANK
            out.append((kb, q, e))
            q = e
    return out


ALL_STEPS = [(g, i) for g in range(NG) for i in range(STEPS)]
STARTS = [sum(len(step_uses(i)) for _, i in ALL_STEPS[:s]) for s in range(len(ALL_STEPS))]
NS = sum(len(step_uses(i)) for _, i in ALL_STEPS)
assert NS % RING == 0


def max_pieces(g, tiles=range(NT)):
    return [("max", h, t, p) for t in tiles for h in range(g * GH, g * GH + GH)
            for p in range((t * P) // BANK + 1)]


PARTS_OF = {"qkv": 2 * NC, "early": 4, "mid": 4, "qT": 4, "kT": 4, "paths": NT // 2 * NJ}


def in_parts(name):
    return [("part", name, k) for k in range(PARTS_OF.get(name[0], 1) - 1)] + [name]


def columns(name):
    part, use = (name[2], name[1]) if name[0] == "part" else (PARTS_OF.get(name[0], 1) - 1, name)
    what = use[0]
    if what == "S":
        return BANK
    if what == "value":
        _, q, e = step_segments(ALL_STEPS[use[1]][1])[use[2]]
        return 4 * (e - q)
    if what == "max":
        return min(BANK, (use[2] + 1) * P - use[3] * BANK)
    return {"qkv": 4 * BANK if part < NC else 4 * D, "early": 4 * BANK, "mid": 4 * BANK, "qT": BANK,
            "kT": BANK, "mask": SLOT, "paths": 4 * D, "cut": 0}.get(what, SLOT)


def step_of(n):
    return max(s for s in range(len(ALL_STEPS)) if STARTS[s] <= n)


def between(main, filler):
    def load(name):
        return columns(name) + FILLER_COST

    out = []
    total, whole = sum(map(columns, main)), sum(map(load, filler))
    done = placed = k = 0
    for name in main:
        out.append(name)
        done += columns(name)
        while k < len(filler) and (done >= total or (placed + load(filler[k]) / 2) * total < done * whole):
            placed += load(filler[k])
            out.append(filler[k])
            k += 1
    return out


def plan_body(beside):
    out = [("onehot",)] + in_parts(("qkv", 3))
    for t in range(NJ):
        qT, kT = in_parts(("qT", t)), in_parts(("kT", t))
        if t + 4 < NT:
            qkv = in_parts(("qkv", t + 4))
            main = qT + qkv + kT + [("mask", t)] + in_parts(("mid", t))
            if t + 2 == NJ:
                main += [("mask", t + 1)]
        else:
            main = qT + kT
        pieces = []
        if t:
            pieces = max_pieces(0, [t - 1]) + max_pieces(1, [t - 1])[:ALONG if t + 4 < NT else ALONG_LAST]
        out += main[:4] + between(main[4:], pieces)
    ffn = in_parts(("paths", 0)) + in_parts(("paths", 1))
    for t in range(NJ, NT):
        main = between(ffn[:BESIDE_TILE], in_parts(("qT", t)) + in_parts(("kT", t)))
        ffn = ffn[BESIDE_TILE:]
        out += main[:4] + between(main[4:], max_pieces(0, [t - 1]))
    second = [x for x in max_pieces(1) if x not in out]
    left = max_pieces(0, [NT - 1])
    for g in range(NG):
        after = second if g == 0 else max_pieces(g + 1) if g + 1 < NG else []
        left += [("cut", g)] + after[:CUT_LAG] + [("shift", g)] + after[CUT_LAG:]
    start = left.index(("cut", 0)) + 2 + EARLY
    out += between(ffn, left[:start])
    rest = left[start:]
    main = []
    for s, (g, i) in enumerate(ALL_STEPS):
        uses = step_uses(i)
        segs = [("value", s - 1, k) for k in range(len(step_segments(ALL_STEPS[s - 1][1])))] if s else []
        for k in range(len(uses)):
            n = STARTS[s] + k
            if n == MAXIMA_END:
                out += between(main, rest)
                main = []
            m = -(-len(segs) // (len(uses) - k)) if k or len(segs) > len(uses) else 0
            main += between([("S", n, 0), ("S", n, 1)], segs[:m])
            segs = segs[m:]
            if g and i == 3 and k == 0:
                main.append(("oT", g - 1))
            main += beside.get(n, [])
    out += main
    s = len(ALL_STEPS) - 1
    out += [("value", s, k) for k in range(len(step_segments(ALL_STEPS[s][1])))]
    return out


LAST_GROUP = NS - NS // NG
BESIDE = {LAST_GROUP + 3: [("xnT", 0)], LAST_GROUP + 5: [("xnT", 1)]}
for tile, slot in ((0, LAST_GROUP + 8), (1, LAST_GROUP + 13)):
    for part, name in enumerate(in_parts(("qkv", tile))):
        BESIDE[slot + part] = [name]
HEAD = sum((BESIDE[n] for n in sorted(BESIDE)), []) + in_parts(("early",)) + [("scores",)] + in_parts(("qkv", 2))
TAIL = [("oT", NG - 1), ("attnT", 0), ("attnT", 1), ("proj", 0), ("proj", 1)]
EARLY_PARTS, QKV_PARTS = in_parts(("early",)), in_parts(("qkv", 2))
BESIDE_BODY = plan_body(BESIDE)
LOOP = (BESIDE_BODY[:-1] + EARLY_PARTS[:2] + BESIDE_BODY[-1:] + EARLY_PARTS[2:3]
        + [("oT", NG - 1)] + EARLY_PARTS[3:]
        + [("attnT", 0), ("attnT", 1), ("scores",)] + QKV_PARTS[:3] + [("proj", 0)] + QKV_PARTS[3:] + [("proj", 1)])
LAST = plan_body({}) + TAIL
assert sorted(map(str, LOOP)) == sorted(map(str, LAST + HEAD))

BY_ACT = {"qkv", "early", "qT", "mask", "shift", "S"}
BY_DVE = {"scores", "onehot", "kT", "mid", "paths", "max", "oT", "proj"}


def taker(name):
    if name in (("xnT", 0), ("attnT", 0)) or name[0] in BY_ACT:
        return "act"
    if name in (("xnT", 1), ("attnT", 1)) or name[0] in BY_DVE:
        return "dve"
    return None


PLACES = {
    "plain": {"large": (2, (0, 2, 4, 6))},
    "maxima": {"large": (2, (0, 2, 6)), "small": (1, (4, 5))},
    "attention": {"scores": (1, (0, 1, 2)), "small": (1, (3, 4, 5)), "large": (2, (4,))},
    "last group": {"scores": (1, (0, 1, 2, 3)), "large": (2, (4,))},
}


class Order:

    def __init__(self, names, previous=None):
        self.names = names
        self.place, self.taken, self.bank, self.before = {}, {}, {}, {}
        self.before_values = None
        self.count = {"act": 0, "dve": 0}
        last = [None] * 8
        if previous:
            last = [(previous.count[taker(x)] - previous.taken[x], x) for _, x in previous.left]
        since = [-1, -1, -3, -3, -2, -2, -4, -4]
        stage = "plain"
        for n, name in enumerate(names):
            use = name[1] if name[0] == "part" else name
            who = taker(use)
            if use == ("qT", 1):
                stage = "maxima"
            elif use[0] == "S" and stage == "maxima":
                stage = "attention"
            elif use == ("oT", NG - 1):
                stage = "plain"
            if use[0] == "value" and self.before_values is None:
                self.before_values = set(last[6:8])
            if who is None:
                continue
            if use not in self.bank:
                width, banks = PLACES[stage]["small" if use[0] in ("max", "shift") else
                                             "scores" if use[0] == "S" else "large"]
                free = [k for k in banks
                        if not last[k] or last[k][0] is not None or last[k][1] in self.place]
                at = min(free, key=since.__getitem__)
                self.bank[use] = at
                self.before[use] = set(last[at:at + width])
                for k in range(at, at + width):
                    last[k] = (None, use)
                    since[k] = n
            if name == ("shift", NG - 1):
                stage = "last group"
            if name is use:
                self.place[use] = len(self.place) + 1
                self.count[who] += 1
                self.taken[use] = self.count[who]
        self.left = last


LOOP_ORDER = Order(LOOP)
ORDERS = {"first": Order(HEAD), "loop": Order(LOOP, LOOP_ORDER), "last": Order(LAST, LOOP_ORDER)}
NU = len(ORDERS["loop"].place)
NTAKEN = ORDERS["loop"].count
TAIL_COUNT = Order(TAIL).count | {"pe": len(Order(TAIL).place)}
SEAM_COUNT = {who: n + (ORDERS["first"].count | {"pe": len(ORDERS["first"].place)})[who]
              for who, n in TAIL_COUNT.items()}
FFN_NORM_AT = 2
FFN_FROM = 10
NORM_AT = 52
FIRST_LINKS, DVE_LINKS = 16, 46


def build(nc, x, wqk, wv, wo, mixk, w1, b1, b1_last, w2, bo1, wo2, bo2, gamma, beta,
          cos_t, sin_t, ident, order, spread, out):
    ctx = ExitStack()
    with ctx:
        def sb(name, shape, dt):
            return ctx.enter_context(nc.sbuf_tensor(name, shape, dt))

        def sem(name):
            return ctx.enter_context(nc.semaphore(name))

        wqk_sb = sb("wqk_sb", [P, NC, 2 * D], F32)
        wv_sb = sb("wv_sb", [P, NC, D], F32)
        wo_sb = sb("wo_sb", [P, NC, D], F32)
        mixk_sb = sb("mixk_sb", [P, NC, 3], F32)
        w1_sb = sb("w1_sb", [P, NC, MID + DM], F32)
        b1_sb = sb("b1_sb", [P, NJ], F32)
        w2_sb = sb("w2_sb", [P, NJ, D], F32)
        wo2_sb = sb("wo2_sb", [P, PATHS], F32)
        bo2_sb = sb("bo2_sb", [P, PATHS], F32)
        gamma_sb = sb("gamma_sb", [P, D], F32)
        beta_sb = sb("beta_sb", [P, D], F32)
        cos_sb = sb("cos_sb", [P, NT, DK], F32)
        sin_sb = sb("sin_sb", [P, NT, DK], F32)
        ident_sb = sb("ident_sb", [P, P], F32)
        ident_bf = sb("ident_bf", [P, P], BF16)
        causal_sb = sb("causal_sb", [P, S], BF16)
        order_sb = sb("order_sb", [P, PATHS], F32)
        xm = sb("xm", [P, NC, S], F32)
        spread_sb = xm[0:PATHS, 0, 0:MID + PATHS]
        spread_bf = sb("spread_bf", [PATHS, MID + PATHS], BF16)
        mhalf = sb("mhalf", [P, NT], F32)
        x_sb = sb("x_sb", [P, NT, D], F32)
        xn = sb("xn", [P, NT, D], F32)
        acc = sb("acc", [P, NT, D], F32)
        xnT = sb("xnT", [P, NC, S + 2], F32)
        shared = sb("shared", [P, NT * D], F32)
        attn = shared[:, :].rearrange("p (t d) -> p t d", d=D)
        stats = sb("stats", [P, NT, 6], F32)
        mv = sb("mv", [P, NT, 2], F32)
        ve = sb("ve", [P, NT], F32)
        rs = sb("rs", [P, NT], F32)
        rt = sb("rt", [P, NT], F32)
        rmax = sb("rmax", [P, NT], F32)
        score_sb = sb("score_sb", [P, NT, PATHS], F32)
        req = sb("req", [P, NT, PATHS], F32)
        onehot = sb("onehot", [P, NT, PATHS], BF16)
        onehotT = sb("onehotT", [PATHS, S], BF16)
        mask = shared[:, 4 * D:8 * D].bitcast(BF16).rearrange("p (i s) -> p i s", i=2)
        q_sb = sb("q_sb", [P, 2, 2 * D], F32)
        rope_b = sb("rope_b", [P, 2, 2 * D], F32)
        roped = shared[:, 0:4 * D].rearrange("p (i d) -> p i d", i=2)
        rest = sb("rest", [P, 2 * D], F32)
        v_sb = sb("v_sb", [P, NT, H, VW], F32)
        qT = sb("qT", [PARTS + SHIFT, H, S], BF16)
        kT = sb("kT", [PARTS + SHIFT, H, S], BF16)
        piecemax = sb("piecemax", [P, NT, H, 2], F32)
        rowmax = sb("rowmax", [P, NT, GH], F32)
        shifts = sb("shifts", [P, NT, 2, GH], BF16)
        shiftT = sb("shiftT", [NSHIFT, S], BF16)
        prob = sb("prob", [P, RING, S], F32)
        mid = prob[:, 0:NJ, :]
        hidden = prob[DM:P, NJ - 1, :]
        parts = prob[:, NJ:RING, :].rearrange("p r s -> p (r s)").bitcast(BF16).rearrange(
            "p (i a h n) -> p i a h n", i=2, a=2, h=H)
        attnT = prob[:, 0:NC, :]
        o_sb = sb("o_sb", [P, S], F32)
        rden = sb("rden", [P, NT, GH], F32)
        slots = [ctx.enter_context(nc.psum_tensor(f"slot{i}", [P, SLOT], F32)) for i in range(4)]
        o_ps = slots[3]

        weights_loaded = sem("weights_loaded")
        consts_set = sem("consts_set")
        gates_passed = sem("gates_passed")
        mhalf_set = sem("mhalf_set")
        ones_set = sem("ones_set")
        kT_ones_set = sem("kT_ones_set")
        x_loaded = sem("x_loaded")
        slot_filled = sem("slot_filled")
        act_took = sem("act_took")
        dve_took = sem("dve_took")
        dve_linked = sem("dve_linked")
        var_ready = sem("var_ready")
        rsqrt_ready = sem("rsqrt_ready")
        xn_ready = sem("xn_ready")
        acc_begun = sem("acc_begun")
        acc_ffn = sem("acc_ffn")
        mixed = sem("mixed")
        routed = sem("routed")
        rope_products = sem("rope_products")
        rope_done = sem("rope_done")
        hi_cut = sem("hi_cut")
        all_cut = sem("all_cut")
        mid_ready = sem("mid_ready")
        normed = sem("normed")
        shift_cut = sem("shift_cut")
        shift_placed = sem("shift_placed")
        masked = sem("masked")
        pv_done = sem("pv_done")
        o_copied = sem("o_copied")
        out_stored = sem("out_stored")
        NWEIGHTS = 19
        NCONSTS = 7

        def gate(eng):
            eng.sem_inc(gates_passed, 1)

        def now(b, per, k):
            return b * per + k

        def batch_of(run, b, t):
            return b + 1 if run == "loop" and t < 3 else b

        def filled(run, b, name):
            o = ORDERS[run].place[name]
            return TAIL_COUNT["pe"] + o if run == "first" else b * NU + SEAM_COUNT["pe"] + o

        def took(run, b, name):
            who = taker(name)
            o = ORDERS[run].taken[name]
            return TAIL_COUNT[who] + o if run == "first" else b * NTAKEN[who] + SEAM_COUNT[who] + o

        def seam_took(b, who):
            return b * NTAKEN[who] + SEAM_COUNT[who]

        def slot_of(run, name):
            k = ORDERS[run].bank[name]
            if name[0] in ("max", "shift", "S"):
                return slots[k // 2][:, k % 2 * BANK:(k % 2 + 1) * BANK]
            return slots[k // 2]

        def every_batch(eng, body):
            with eng.Fori(0, B - 1) as b:
                body("loop", b)
            body("last", B - 1)

        block = ctx.enter_context(nc.Block())

        @block.sync
        def _(sp):
            def load_x(b):
                sp.dma_start(x_sb[:, :, :], x[bass.ds(b, 1)].rearrange("a (t p) d -> p (a t) d", p=P)
                             ).then_inc(x_loaded, 16)

            load_x(0)
            sp.dma_start(ident_sb[:, :], ident).then_inc(weights_loaded, 16)
            sp.dma_start(gamma_sb[:, :], gamma.partition_broadcast(P)).then_inc(weights_loaded, 16)
            sp.dma_start(beta_sb[:, :], beta.partition_broadcast(P)).then_inc(weights_loaded, 16)
            for dst, src in ((mixk_sb, mixk), (wqk_sb, wqk), (wv_sb, wv),
                             (cos_sb, cos_t), (sin_sb, sin_t), (w1_sb, w1), (wo_sb, wo)):
                sp.dma_start(dst[:, :, :], src).then_inc(weights_loaded, 16)
            sp.dma_start(b1_sb[DM:P, NJ - 1:NJ], bo1).then_inc(weights_loaded, 16)
            sp.dma_start(wo2_sb[DM:P, :], wo2).then_inc(weights_loaded, 16)
            sp.dma_start(bo2_sb[:, :], bo2.partition_broadcast(P)).then_inc(weights_loaded, 16)
            sp.dma_start(b1_sb[:, 0:NJ - 1], b1).then_inc(weights_loaded, 16)
            sp.dma_start(b1_sb[0:DM, NJ - 1:NJ], b1_last).then_inc(weights_loaded, 16)
            sp.dma_start(w2_sb[:, 0:NJ - 1, :], w2[0:P * (NJ - 1)].rearrange("(j p) d -> p j d", p=P)
                         ).then_inc(weights_loaded, 16)
            sp.dma_start(w2_sb[0:LAST_ROWS, NJ - 1, :], w2[P * (NJ - 1):MID + PATHS]).then_inc(weights_loaded, 16)
            sp.dma_start(spread_sb, spread).then_inc(weights_loaded, 16)
            sp.dma_start(order_sb[:, :], order).then_inc(weights_loaded, 16)

            def place_shift(run, b, g):
                sp.wait_ge(act_took, took(run, b, ("shift", g)))
                for k in range(SHIFT):
                    sp.dma_start(qT[PARTS + k:PARTS + k + 1, g * GH:(g + 1) * GH, :],
                                 shiftT[k * GH:(k + 1) * GH, :]).then_inc(shift_placed, 16)

            def store(run, b):
                for i in range(2):
                    sp.wait_ge(dve_took, took(run, b, ("proj", i)))
                    sp.dma_start(out[bass.ds(b, 1), i * S // 2:(i + 1) * S // 2, :]
                                 .rearrange("a (t p) d -> p (a t) d", p=P),
                                 acc[:, i * NT // 2:(i + 1) * NT // 2, :]).then_inc(out_stored, 16)

            def body(run, b):
                if run == "loop":
                    sp.wait_ge(acc_begun, now(b, 1, 1))
                    load_x(b + 1)
                for g in range(NG):
                    place_shift(run, b, g)
                store(run, b)

            every_batch(sp, body)
            sp.wait_ge(out_stored, 32 * B + 32)

        @block.gpsimd
        def _(pool):
            def rsqrt(value):
                pool.wait_ge(var_ready, value)
                nc.gpsimd.tensor_tensor(rs[:, :], ve[:, :], mhalf[:, :], ALU.pow).then_inc(rsqrt_ready, 1)

            made = [0]

            def make(ins):
                made[0] += 1
                ins.then_inc(consts_set, 1)
                pool.wait_ge(consts_set, made[0])

            nc.gpsimd.memset(mhalf[:, :], -0.5).then_inc(mhalf_set, 1)
            make(nc.gpsimd.memset(xnT[:, :, 0:S + 2:S + 1], 0.0))
            make(nc.gpsimd.memset(v_sb[:, :, :, DK:VW], 0.0))
            make(nc.gpsimd.memset(v_sb[:, :, :, DK:DK + 1], 1.0))
            make(nc.gpsimd.memset(causal_sb[:, :], 0.0))
            make(nc.gpsimd.affine_select(out=causal_sb[:, S - P:], in_=causal_sb[:, S - P:],
                                         compare_op=ALU.is_ge, fill=NEG, base=0, pattern=[[-1, P]],
                                         channel_multiplier=1))
            pool.wait_ge(mhalf_set, 1)
            rsqrt(1)
            pool.wait_ge(weights_loaded, 16 * NWEIGHTS)
            make(nc.gpsimd.tensor_copy(ident_bf[:, :], ident_sb[:, :]))
            make(nc.gpsimd.tensor_copy(spread_bf[:, :], spread_sb))
            assert made[0] == NCONSTS
            pool.sem_inc(out_stored, 32)

            def rotate(run, b, t):
                batch = batch_of(run, b, t)
                pool.wait_ge(act_took, took(run, b, ("qkv", t)))
                q4 = q_sb[:, t % 2, :].rearrange("p (h d) -> p h d", d=DK)
                r4 = rope_b[:, t % 2, :].rearrange("p (h d) -> p h d", d=DK)
                hd = DK // 2
                for a, z in ((0, hd), (hd, 0)):
                    ins = nc.gpsimd.tensor_tensor(
                        r4[:, :, a:a + hd], q4[:, :, z:z + hd],
                        sin_sb[:, t, None, a:a + hd].to_broadcast([P, 2 * H, hd]), ALU.mult)
                ins.then_inc(rope_products, 1)
                if t >= 2:
                    pool.wait_ge(all_cut, now(batch, NT, t - 1))
                elif run == "loop":
                    pool.wait_ge(slot_filled, filled(run, b, ("attnT", 1)))
                nc.gpsimd.tensor_tensor(roped[:, t % 2, :].rearrange("p (h d) -> p h d", d=DK), q4,
                                        cos_sb[:, t, None, :].to_broadcast([P, 2 * H, DK]),
                                        ALU.mult).then_inc(rope_products, 1)
                pool.wait_ge(rope_products, now(batch, 2 * NT, 2 * (t + 1)))
                nc.gpsimd.tensor_tensor(roped[:, t % 2, :], roped[:, t % 2, :], rope_b[:, t % 2, :],
                                        ALU.add).then_inc(rope_done, 1)

            def add_ffn(b, k):
                t, step = k // 3, k % 3
                if k == 0:
                    pool.wait_ge(normed, now(b, 1, 1))
                    gate(pool)
                if step:
                    pool.wait_ge(acc_ffn, now(b, 3 * NT, k))
                y, a = xn[:, t, :], acc[:, t, :]
                if step == 0:
                    ins = nc.gpsimd.tensor_scalar(y, y, mv[:, t, 0:1], rt[:, t:t + 1], ALU.subtract, ALU.mult)
                elif step == 1:
                    ins = nc.gpsimd.tensor_tensor(y, y, gamma_sb[:, :], ALU.mult)
                else:
                    ins = nc.gpsimd.tensor_tensor(a, a, y, ALU.add)
                ins.then_inc(acc_ffn, 1)

            def mask_diagonal(run, b, s, k):
                n = STARTS[s] + k
                pool.wait_ge(act_took, took(run, b, ("S", n, 1)))
                gate(pool)
                for _, _, c, _ in step_uses(ALL_STEPS[s][1])[k]:
                    d = prob[:, n % RING, c:c + P]
                    ins = nc.gpsimd.affine_select(out=d, in_=d, compare_op=ALU.is_ge, fill=0.0, base=0,
                                                  pattern=[[1, P]], channel_multiplier=-1)
                ins.then_inc(masked, 1)

            def body(run, b):
                for t in range(3, NT):
                    rotate(run, b, t)
                    if t == NT // 2:
                        pool.wait_ge(out_stored, now(b, 32, 32))
                        nc.gpsimd.tensor_tensor(acc[:, :, :], x_sb[:, :, :],
                                                beta_sb[:, None, :].to_broadcast([P, NT, D]),
                                                ALU.add).then_inc(acc_begun, 1)
                rsqrt(now(b, 2, 2))
                for s, (_, i) in enumerate(ALL_STEPS):
                    for k in range(len(step_uses(i))):
                        mask_diagonal(run, b, s, k)
                        n = STARTS[s] + k
                        if FFN_FROM <= n < FFN_FROM + 3 * NT:
                            add_ffn(b, n - FFN_FROM)
                        if run == "loop" and n == NORM_AT:
                            rsqrt(now(b, 2, 3))
                if run == "loop":
                    for t in range(3):
                        rotate(run, b, t)

            for t in range(3):
                rotate("first", 0, t)
            every_batch(pool, body)

        @block.scalar
        def _(act):
            act.sem_inc(act_took, TAIL_COUNT["act"])
            act.wait_ge(mhalf_set, 1)
            nc.scalar.mul(kT[PARTS:PARTS + SHIFT, :, :],
                          mhalf[PARTS:PARTS + SHIFT, None, 0:1].to_broadcast([SHIFT, H, S]), -2.0
                          ).then_inc(kT_ones_set, 1)
            act.wait_ge(weights_loaded, 16 * NWEIGHTS)
            act.wait_ge(consts_set, NCONSTS)

            def take(run, b, name):
                act.wait_ge(slot_filled, filled(run, b, name))
                return slot_of(run, name)

            def copy_turned(run, b, name):
                ps = take(run, b, name)
                dst = xnT[:, 0, 1:S + 1] if name[0] == "xnT" else attnT[:, 0, :]
                nc.scalar.copy(dst, ps[:, :]).then_inc(act_took, 1)

            def copy_qkv(run, b, t):
                if t >= 2:
                    act.wait_ge(rope_done, now(batch_of(run, b, t), NT, t - 1))
                elif run == "loop":
                    act.wait_ge(pv_done, now(b, len(ALL_STEPS), len(ALL_STEPS) - STEPS + t + 1))
                ps = take(run, b, ("qkv", t))
                nc.scalar.copy(q_sb[:, t % 2, :], ps[:, 0:2 * D])
                nc.scalar.copy(v_sb[:, t, :, 0:DK],
                               ps[:, 2 * D:3 * D].rearrange("p (h d) -> p h d", d=DK)
                               ).then_inc(act_took, 1)

            def cut_hi(run, b, t):
                act.wait_ge(rope_done, now(b, NT, t + 1))
                if t >= 2:
                    act.wait_ge(slot_filled, filled(run, b, ("kT", t - 2)))
                pt = parts[:, t % 2, :, :, :].rearrange("p a h (n d) -> p a h n d", d=DK)
                r = roped[:, t % 2, :].rearrange("p (a h d) -> p a h d", a=2, d=DK)
                nc.scalar.copy(pt[:, 0, :, 0:6:3, :], r[:, 0, :, None, :].to_broadcast([P, H, 2, DK]))
                nc.scalar.copy(pt[:, 0, :, 5, :], r[:, 0, :, :])
                nc.scalar.copy(pt[:, 1, :, 0:3, :], r[:, 1, :, None, :].to_broadcast([P, H, 3, DK])
                               ).then_inc(hi_cut, 1)

            def copy_qT(run, b, t):
                ps = take(run, b, ("qT", t))
                nc.scalar.copy(qT[0:PARTS, :, t * P:(t + 1) * P],
                               ps[0:PARTS, :].bitcast(BF16).rearrange("p (h c) -> p h c", c=P)
                               ).then_inc(act_took, 1)

            def activate_early(run, b):
                if run == "loop":
                    act.wait_ge(pv_done, now(b, len(ALL_STEPS), len(ALL_STEPS)))
                ps = take(run, b, ("early",))
                nc.scalar.activation(hidden, ps[DM:P, :], ACT.Tanh, bias=b1_sb[DM:P, NJ - 1:NJ])
                nc.scalar.activation(mid[0:DM, NJ - 1, :], ps[0:DM, :], ACT.Identity,
                                     bias=b1_sb[0:DM, NJ - 1:NJ]).then_inc(act_took, 1)

            def copy_mask(run, b, j):
                if j >= 2:
                    act.wait_ge(dve_took, took(run, b, ("mid", j - 2)))
                ps = take(run, b, ("mask", j))
                rows = P if j < NJ - 1 else LAST_ROWS
                nc.scalar.copy(mask[0:rows, j % 2, :], ps[0:rows, :]).then_inc(act_took, 1)

            def copy_shift(run, b, g):
                if g:
                    act.wait_ge(shift_placed, now(b, 32 * NG, 32 * g))
                ps = take(run, b, ("shift", g))
                nc.scalar.copy(shiftT[:, :], ps[0:NSHIFT, :].bitcast(BF16)).then_inc(act_took, 1)

            def copy_sums(run, b, g):
                act.wait_ge(pv_done, now(b, len(ALL_STEPS), STEPS * (g + 1)))
                if g:
                    act.wait_ge(slot_filled, filled(run, b, ("oT", g - 1)))
                nc.scalar.copy(o_sb[:, :], o_ps[:, :]).then_inc(o_copied, 1)

            def exponentiate(run, b, n, half):
                if n >= RING and half == 0:
                    act.wait_ge(pv_done, now(b, len(ALL_STEPS), step_of(n - RING) + 1))
                ps = take(run, b, ("S", n, half))
                nc.scalar.activation(prob[:, n % RING, half * BANK:(half + 1) * BANK], ps[:, :], ACT.Exp,
                                     scale=float(DK) ** -0.5).then_inc(act_took, 1)

            def walk(run, b, names):
                for name in names:
                    what = name[0]
                    if what == "qkv":
                        copy_qkv(run, b, name[1])
                    elif name in (("xnT", 0), ("attnT", 0)):
                        copy_turned(run, b, name)
                        if what == "attnT" and run == "loop":
                            cut_hi(run, b + 1, 0)
                            cut_hi(run, b + 1, 1)
                    elif what == "early":
                        activate_early(run, b)
                        if run == "first":
                            cut_hi(run, b, 0)
                            cut_hi(run, b, 1)
                    elif what == "qT":
                        copy_qT(run, b, name[1])
                        if name[1] in (NJ - 1, NJ):
                            cut_hi(run, b, name[1] + 2)
                    elif what == "mask":
                        copy_mask(run, b, name[1])
                        if name[1] < NJ - 1:
                            cut_hi(run, b, name[1] + 2)
                    elif what == "shift":
                        copy_shift(run, b, name[1])
                    elif what == "S":
                        exponentiate(run, b, name[1], name[2])
                    elif what == "value":
                        g, i = ALL_STEPS[name[1]]
                        if i == STEPS - 1 and name[2] == len(step_segments(i)) - 1:
                            copy_sums(run, b, g)

            walk("first", 0, HEAD)
            every_batch(act, lambda run, b: walk(run, b, ORDERS[run].names))

        @block.vector
        def _(dve):
            dve.sem_inc(dve_took, TAIL_COUNT["dve"])
            nc.vector.memset(piecemax[:, :, :, :], NEG).then_inc(ones_set, 1)
            dve.wait_ge(ones_set, 1)
            links = {"first": 0, "loop": 0, "last": 0}

            def link(run, b, ins):
                links[run] += 1
                ins.then_inc(dve_linked, 1)
                dve.wait_ge(dve_linked, links[run] if run == "first" else
                            FIRST_LINKS + now(b, DVE_LINKS, links[run]))

            def take(run, b, name):
                dve.wait_ge(slot_filled, filled(run, b, name))
                return slot_of(run, name)

            def norm_stats(run, b, src):
                for t in range(NT):
                    ins = nc.vector.bn_stats(stats[:, t, :], src[:, t, :])
                link(run, b, ins)
                gate(dve)
                for t in range(NT):
                    ins = nc.vector.bn_aggr(mv[:, t, :], stats[:, t, :])
                link(run, b, ins)
                nc.vector.tensor_scalar(ve[:, :], mv[:, :, 1], EPS, None, ALU.add).then_inc(var_ready, 1)

            def norm_root(run, b, value):
                dve.wait_ge(rsqrt_ready, value)
                link(run, b, nc.vector.tensor_tensor(rt[:, :], rs[:, :], rs[:, :], ALU.mult))
                link(run, b, nc.vector.tensor_tensor(rt[:, :], rt[:, :], ve[:, :], ALU.mult))
                link(run, b, nc.vector.tensor_scalar(rt[:, :], rt[:, :], -0.5, 1.5, ALU.mult, ALU.add))
                link(run, b, nc.vector.tensor_tensor(rt[:, :], rs[:, :], rt[:, :], ALU.mult))

            def normalize(dst, src, signal):
                for t in range(NT):
                    nc.vector.tensor_scalar(dst[:, t, :], src[:, t, :], mv[:, t, 0:1], rt[:, t:t + 1],
                                            ALU.subtract, ALU.mult).then_inc(signal, 1)

            def copy_turned(run, b, name):
                ps = take(run, b, name)
                dst = xnT[:, 1, 1:S + 1] if name[0] == "xnT" else attnT[:, 1, :]
                nc.vector.tensor_copy(dst, ps[:, :]).then_inc(dve_took, 1)

            def mix(run, b):
                dve.wait_ge(act_took, took(run, b, ("xnT", 0)))
                dve.wait_ge(dve_took, took(run, b, ("xnT", 1)))
                for k in range(3):
                    for c in range(NC):
                        if k == 0:
                            ins = nc.vector.tensor_scalar(xm[:, c, :], xnT[:, c, 0:S], mixk_sb[:, c, 0:1],
                                                          None, ALU.mult)
                        else:
                            ins = nc.vector.scalar_tensor_tensor(xm[:, c, :], xnT[:, c, k:k + S],
                                                                 mixk_sb[:, c, k:k + 1], xm[:, c, :],
                                                                 ALU.mult, ALU.add)
                    if k < 2:
                        link(run, b, ins)
                ins.then_inc(mixed, 1)

            def cut_rest(run, b, t):
                batch = b + 1 if run == "loop" and t < 2 else b
                dve.wait_ge(hi_cut, now(batch, NT, t + 1))
                if t:
                    dve.wait_ge(all_cut, now(batch, NT, t))
                pt = parts[:, t % 2, :, :, :].rearrange("p a h (n d) -> p a h n d", d=DK)
                r = roped[:, t % 2, :].rearrange("p (a h d) -> p a h d", a=2, d=DK)
                e = rest[:, :].rearrange("p (a h d) -> p a h d", a=2, d=DK)
                link(run, b, nc.vector.tensor_tensor(e, r, pt[:, :, :, 0, :], ALU.subtract))
                nc.vector.tensor_copy(pt[:, 0, :, 1:5:3, :], e[:, 0, :, None, :].to_broadcast([P, H, 2, DK]))
                link(run, b, nc.vector.tensor_copy(pt[:, 1, :, 3:5, :],
                                                   e[:, 1, :, None, :].to_broadcast([P, H, 2, DK])))
                nc.vector.tensor_tensor(pt[:, 0, :, 2, :], e[:, 0], pt[:, 0, :, 1, :], ALU.subtract)
                nc.vector.tensor_tensor(pt[:, 1, :, 5, :], e[:, 1], pt[:, 1, :, 3, :],
                                        ALU.subtract).then_inc(all_cut, 1)

            def copy_kT(run, b, t):
                ps = take(run, b, ("kT", t))
                nc.vector.tensor_copy(kT[0:PARTS, :, t * P:(t + 1) * P],
                                      ps[0:PARTS, :].bitcast(BF16).rearrange("p (h c) -> p h c", c=P)
                                      ).then_inc(dve_took, 1)

            def route(run, b):
                ps = take(run, b, ("scores",))
                tiles = [P, NT, PATHS]
                nc.vector.tensor_tensor(score_sb[:, :, :],
                                        ps[:, 0:NT * PATHS].rearrange("p (t n) -> p t n", n=PATHS),
                                        bo2_sb[:, None, :].to_broadcast(tiles), ALU.add).then_inc(dve_took, 1)
                dve.wait_ge(dve_took, took(run, b, ("scores",)))
                link(run, b, nc.vector.tensor_reduce(rmax[:, :], score_sb[:, :, :], AX.X, ALU.max))
                top = rmax[:, :, None].to_broadcast(tiles)
                link(run, b, nc.vector.tensor_tensor(req[:, :, :], score_sb[:, :, :], top, ALU.is_equal))
                link(run, b, nc.vector.tensor_tensor(req[:, :, :], req[:, :, :],
                                                     order_sb[:, None, :].to_broadcast(tiles), ALU.mult))
                link(run, b, nc.vector.tensor_reduce(rmax[:, :], req[:, :, :], AX.X, ALU.max))
                nc.vector.tensor_tensor(onehot[:, :, :], req[:, :, :], top, ALU.is_equal).then_inc(routed, 1)

            def copy_onehotT(run, b):
                ps = take(run, b, ("onehot",))
                nc.vector.tensor_copy(onehotT[:, :], ps[0:PATHS, 0:BANK].bitcast(BF16)
                                      ).then_inc(dve_took, 1)

            def select_mid(run, b, j):
                dve.wait_ge(act_took, took(run, b, ("mask", j)))
                ps = take(run, b, ("mid", j))
                nc.vector.scalar_tensor_tensor(mid[:, j, :], ps[:, :], b1_sb[:, j:j + 1], mask[:, j % 2, :],
                                               ALU.add, ALU.mult).then_inc(dve_took, 1)

            def select_last(run, b):
                dve.wait_ge(act_took, took(run, b, ("mask", NJ - 1)))
                m = mask[:, (NJ - 1) % 2, :]
                nc.vector.tensor_copy(mid[DM:LAST_ROWS, NJ - 1, :], m[DM:LAST_ROWS, :])
                nc.vector.tensor_tensor(mid[0:DM, NJ - 1, :], mid[0:DM, NJ - 1, :], m[0:DM, :],
                                        ALU.mult).then_inc(mid_ready, 1)

            def add_paths(run, b, i):
                ps = take(run, b, ("paths", i))
                y = xn[:, i * NT // 2:(i + 1) * NT // 2, :]
                nc.vector.tensor_tensor(y, ps[:, :].rearrange("p (t d) -> p t d", d=D), y,
                                        ALU.add).then_inc(dve_took, 1)
                if i:
                    dve.wait_ge(dve_took, took(run, b, ("paths", 1)))
                    norm_stats(run, b, xn)

            def max_piece(run, b, h, t, p):
                ps = take(run, b, ("max", h, t, p))
                gate(dve)
                end = (t + 1) * P
                w = min(BANK, end - p * BANK)
                at = S - end + p * BANK
                nc.vector.tensor_tensor_reduce(ps[:, 0:w], ps[:, 0:w], causal_sb[:, at:at + w],
                                               1.0, NEG, ALU.add, ALU.max,
                                               piecemax[:, t, h, p:p + 1]).then_inc(dve_took, 1)

            def cut_shift(run, b, g):
                dve.wait_ge(dve_took, took(run, b, max_pieces(g)[-1]))
                link(run, b, nc.vector.tensor_reduce(rowmax[:, :, :], piecemax[:, :, g * GH:(g + 1) * GH, :],
                                                     AX.X, ALU.max))
                link(run, b, nc.vector.tensor_scalar(shifts[:, :, 0, :], rowmax[:, :, :], -1.0, None, ALU.mult))
                nc.vector.scalar_tensor_tensor(shifts[:, :, 1, :], rowmax[:, :, :], -1.0, shifts[:, :, 0, :],
                                               ALU.mult, ALU.subtract).then_inc(shift_cut, 1)

            def divide_sums(run, b, g):
                if g:
                    dve.wait_ge(dve_took, took(run, b, ("oT", g - 1)))
                ps = take(run, b, ("oT", g))
                o4 = ps[:, :].rearrange("p (t h v) -> p t h v", h=GH, v=VW)
                link(run, b, nc.vector.reciprocal(rden[:, :, :], o4[:, :, :, DK]))
                nc.vector.tensor_tensor(
                    attn[:, :, g * GH * DK:(g + 1) * GH * DK].rearrange("p t (h d) -> p t h d", d=DK),
                    o4[:, :, :, 0:DK], rden[:, :, :, None].to_broadcast([P, NT, GH, DK]),
                    ALU.mult).then_inc(dve_took, 1)

            def finish(run, b, i):
                if i == 0:
                    dve.wait_ge(acc_ffn, now(b, 3 * NT, 3 * NT))
                ps = take(run, b, ("proj", i))
                a = acc[:, i * NT // 2:(i + 1) * NT // 2, :]
                nc.vector.tensor_tensor(a, ps[:, :].rearrange("p (t d) -> p t d", d=D), a,
                                        ALU.add).then_inc(dve_took, 1)

            def walk(run, b, names):
                for name in names:
                    what = name[0]
                    if name in (("xnT", 1), ("attnT", 1)):
                        copy_turned(run, b, name)
                        if what == "xnT" and run == "first":
                            mix(run, b)
                    elif what == "scores":
                        route(run, b)
                        cut_rest(run, b, 0)
                    elif what == "onehot":
                        copy_onehotT(run, b)
                    elif what == "kT":
                        copy_kT(run, b, name[1])
                        if name[1] in (NJ - 1, NJ):
                            cut_rest(run, b, name[1] + 2)
                    elif what == "mid":
                        select_mid(run, b, name[1])
                        cut_rest(run, b, name[1] + 2)
                    elif what == "mask" and name[1] == NJ - 1:
                        select_last(run, b)
                    elif what == "paths":
                        add_paths(run, b, name[1])
                    elif what == "max":
                        max_piece(run, b, *name[1:])
                    elif what == "cut":
                        cut_shift(run, b, name[1])
                    elif name == ("S", FFN_NORM_AT, 0):
                        norm_root(run, b, now(b, 2, 2))
                        dve.sem_inc(normed, 1)
                    elif run == "loop" and name == ("S", NORM_AT, 0):
                        dve.wait_ge(x_loaded, 16 * (b + 2))
                        dve.wait_ge(acc_ffn, now(b, 3 * NT, 3 * NT))
                        norm_stats(run, b, x_sb)
                        norm_root(run, b, now(b, 2, 3))
                        normalize(xn, x_sb, xn_ready)
                    elif what == "oT":
                        divide_sums(run, b, name[1])
                        if name[1] == NG - 2 and run == "loop":
                            mix(run, b)
                    elif what == "proj":
                        finish(run, b, name[1])
                        if name[1] == 0 and run == "loop":
                            cut_rest(run, b, 1)

            dve.wait_ge(x_loaded, 16)
            norm_stats("first", 0, x_sb)
            norm_root("first", 0, 1)
            normalize(xn, x_sb, xn_ready)
            dve.wait_ge(weights_loaded, 16 * NWEIGHTS)
            dve.wait_ge(consts_set, NCONSTS)
            walk("first", 0, HEAD)
            cut_rest("first", 0, 1)
            assert links["first"] == FIRST_LINKS, links
            every_batch(dve, lambda run, b: walk(run, b, ORDERS[run].names))
            assert links["loop"] == DVE_LINKS, links

        @block.tensor
        def _(pe):
            pe.wait_ge(weights_loaded, 16 * NWEIGHTS)
            pe.wait_ge(consts_set, NCONSTS)
            pe.sem_inc(slot_filled, TAIL_COUNT["pe"])

            def begin(run, b, name):
                free_place(run, b, ORDERS[run].before[name])
                return slot_of(run, name)

            def free_place(run, b, before):
                need = {}
                for ago, old in before - {None}:
                    who = taker(old)
                    o = ORDERS[run].taken[old] if ago is None else -ago
                    need[who] = max(need.get(who, o), o)
                for who, o in need.items():
                    base = TAIL_COUNT[who] if run == "first" else b * NTAKEN[who] + SEAM_COUNT[who]
                    pe.wait_ge(act_took if who == "act" else dve_took, base + o)

            def turn(run, b, name):
                what, c = name
                if name == ("xnT", 0):
                    pe.wait_ge(xn_ready, NT if run == "first" else now(b + 1, NT, NT))
                if name == ("attnT", 0):
                    pe.wait_ge(dve_took, took(run, b, ("oT", NG - 1)))
                if what == "oT":
                    pe.wait_ge(o_copied, now(b, NG, c + 1))
                ps = begin(run, b, name)
                for t in range(NT):
                    if what == "oT":
                        src = o_sb[:, t * P:(t + 1) * P]
                    else:
                        src = (xn if what == "xnT" else attn)[:, t, c * P:(c + 1) * P]
                    ins = nc.tensor.transpose(ps[:, t * P:(t + 1) * P], src, ident_sb[:, :])
                ins.then_inc(slot_filled, 1)

            def project(run, b, name, k):
                ps = begin(run, b, name) if k == 0 else slot_of(run, name)
                t = name[1]
                if t == 0 and k == 0:
                    pe.wait_ge(act_took, took(run, b, ("xnT", 0)))
                    pe.wait_ge(dve_took, took(run, b, ("xnT", 1)))
                w, a, n = ((wqk_sb, 0, 2 * D), (wv_sb, 2 * D, D))[k // NC]
                c = k % NC
                return nc.tensor.matmul(ps[:, a:a + n], xnT[:, c, 1 + t * P:1 + (t + 1) * P], w[:, c, :],
                                        start=(c == 0), stop=(c == NC - 1))

            def middle(run, b, name, k):
                ps = begin(run, b, name) if k == 0 else slot_of(run, name)
                j = NJ - 1 if name[0] == "early" else name[1]
                if name[0] == "early" and k == 0:
                    pe.wait_ge(mixed, 1 if run == "first" else now(b + 1, 1, 1))
                n, c = k // NC * BANK, k % NC
                return nc.tensor.matmul(ps[:, n:n + BANK], w1_sb[:, c, j * P:(j + 1) * P],
                                        xm[:, c, n:n + BANK], start=(c == 0), stop=(c == NC - 1))

            def router_scores(run, b):
                ps = begin(run, b, ("scores",))
                pe.wait_ge(act_took, took(run, b, ("early",)))
                for t in range(NT):
                    ins = nc.tensor.matmul(ps[:, t * PATHS:(t + 1) * PATHS], hidden[:, t * P:(t + 1) * P],
                                           wo2_sb[DM:P, :], start=True, stop=True)
                ins.then_inc(slot_filled, 1)

            def turn_onehot(run, b):
                pe.wait_ge(routed, now(b, 1, 1))
                view = begin(run, b, ("onehot",))[0:PATHS, 0:BANK].bitcast(BF16)
                for t in range(NT):
                    ins = nc.tensor.transpose(view[:, t * P:(t + 1) * P], onehot[:, t, :], ident_bf[:, :])
                ins.then_inc(slot_filled, 1)

            def spread_mask(run, b, j):
                ps = begin(run, b, ("mask", j))
                if j == 0:
                    pe.wait_ge(dve_took, took(run, b, ("onehot",)))
                rows = P if j < NJ - 1 else LAST_ROWS
                for n in range(0, S, BANK):
                    ins = nc.tensor.matmul(ps[0:rows, n:n + BANK], spread_bf[:, j * P:j * P + rows],
                                           onehotT[:, n:n + BANK], start=True, stop=True)
                ins.then_inc(slot_filled, 1)

            def turn_parts(run, b, name, k):
                what, t = name
                ps = begin(run, b, name) if k == 0 else slot_of(run, name)
                if what == "qT" and k == 0:
                    pe.wait_ge(all_cut, now(b, NT, t + 1))
                view = ps[0:PARTS, :].bitcast(BF16)
                for h in range(k * H // 4, (k + 1) * H // 4):
                    ins = nc.tensor.transpose(view[:, h * P:(h + 1) * P],
                                              parts[:, t % 2, 0 if what == "qT" else 1, h, :], ident_bf[:, :])
                return ins

            def paths_out(run, b, name, k):
                ps = begin(run, b, name) if k == 0 else slot_of(run, name)
                if name[1] == 0 and k == 0:
                    pe.wait_ge(dve_took, took(run, b, ("mid", NJ - 2)))
                    pe.wait_ge(mid_ready, now(b, 1, 1))
                m, j = k // NJ, k % NJ
                t = name[1] * NT // 2 + m
                rows = P if j < NJ - 1 else LAST_ROWS
                return nc.tensor.matmul(ps[:, m * D:(m + 1) * D], mid[0:rows, j, t * P:(t + 1) * P],
                                        w2_sb[0:rows, j, :], start=(j == 0), stop=(j == NJ - 1))

            def max_scores(run, b, h, t, p):
                if h % GH == 0 and p == 0 and h == 0:
                    pe.wait_ge(act_took, took(run, b, ("qT", t)))
                    pe.wait_ge(dve_took, took(run, b, ("kT", t)))
                ps = begin(run, b, ("max", h, t, p))
                w = min(BANK, (t + 1) * P - p * BANK)
                nc.tensor.matmul(ps[:, 0:w], qT[0:PARTS, h, t * P:(t + 1) * P],
                                 kT[0:PARTS, h, p * BANK:p * BANK + w],
                                 start=True, stop=True).then_inc(slot_filled, 1)

            def turn_shift(run, b, g):
                pe.wait_ge(shift_cut, now(b, NG, g + 1))
                ps = begin(run, b, ("shift", g))
                view = ps[0:NSHIFT, :].bitcast(BF16)
                for t in range(NT):
                    ins = nc.tensor.transpose(view[:, t * P:(t + 1) * P],
                                              shifts[:, t, :, :].rearrange("p a h -> p (a h)"), ident_bf[:, :])
                ins.then_inc(slot_filled, 1)

            def score(run, b, name):
                _, n, half = name
                s = step_of(n)
                k = n - STARTS[s]
                g, i = ALL_STEPS[s]
                if i == 0 and k == 0 and half == 0:
                    pe.wait_ge(shift_placed, now(b, 32 * NG, 32 * (g + 1)))
                ps = begin(run, b, name)
                for hh, kb, c0, w in step_uses(i)[k]:
                    h = g * GH + hh
                    c, e = max(c0, half * BANK), min(c0 + w, (half + 1) * BANK)
                    if c < e:
                        q = kb * P + c - c0
                        ins = nc.tensor.matmul(ps[:, c - half * BANK:e - half * BANK],
                                               kT[:, h, kb * P:(kb + 1) * P],
                                               qT[:, h, q:q + e - c], start=True, stop=True)
                ins.then_inc(slot_filled, 1)

            def values(run, b, s, k):
                g, i = ALL_STEPS[s]
                uses, segments = step_uses(i), step_segments(i)
                if k == 0:
                    pe.wait_ge(masked, now(b, NS, STARTS[s] + len(uses)))
                    if i == 0 and g == 0:
                        free_place(run, b, ORDERS[run].before_values)
                    elif i == 0:
                        pe.wait_ge(o_copied, now(b, NG, g))
                kb, q, e = segments[k]
                where = {hh: (n, c0) for n, blocks in enumerate(uses) for hh, kk, c0, _ in blocks if kk == kb}
                for hh in range(GH):
                    n, c0 = where[hh]
                    c = c0 + q - kb * P
                    ins = nc.tensor.matmul(o_ps[VW * hh:VW * (hh + 1), q:e], v_sb[:, kb, g * GH + hh, :],
                                           prob[:, (STARTS[s] + n) % RING, c:c + e - q],
                                           start=(kb == 0), stop=(kb == (NT // 2 if q >= BANK else NT // 2 - 1)))
                if k == len(segments) - 1:
                    ins.then_inc(pv_done, 1)

            def out_project(run, b, i):
                ps = begin(run, b, ("proj", i))
                if i == 0:
                    pe.wait_ge(act_took, took(run, b, ("attnT", 0)))
                    pe.wait_ge(dve_took, took(run, b, ("attnT", 1)))
                for k in range(NT // 2):
                    t = i * NT // 2 + k
                    for c in range(NC):
                        ins = nc.tensor.matmul(ps[:, k * D:(k + 1) * D], attnT[:, c, t * P:(t + 1) * P],
                                               wo_sb[:, c, :], start=(c == 0), stop=(c == NC - 1))
                ins.then_inc(slot_filled, 1)

            def walk(run, b, names):
                for name in names:
                    what = name[0]
                    use, k = name[1:] if what == "part" else (name, PARTS_OF.get(what, 1) - 1)
                    if use[0] in PARTS_OF:
                        write = {"qkv": project, "early": middle, "mid": middle, "qT": turn_parts,
                                 "kT": turn_parts, "paths": paths_out}[use[0]]
                        ins = write(run, b, use, k)
                        if what != "part":
                            ins.then_inc(slot_filled, 1)
                    elif what in ("xnT", "oT", "attnT"):
                        turn(run, b, name)
                    elif what == "scores":
                        router_scores(run, b)
                    elif what == "onehot":
                        turn_onehot(run, b)
                    elif what == "mask":
                        spread_mask(run, b, name[1])
                    elif what == "max":
                        max_scores(run, b, *name[1:])
                    elif what == "shift":
                        turn_shift(run, b, name[1])
                    elif what == "S":
                        score(run, b, name)
                    elif what == "value":
                        values(run, b, *name[1:])
                    elif what == "proj":
                        out_project(run, b, name[1])

            walk("first", 0, HEAD)
            pe.wait_ge(kT_ones_set, 1)
            pe.wait_ge(act_took, seam_took(0, "act"))
            pe.wait_ge(dve_took, seam_took(0, "dve"))
            every_batch(pe, lambda run, b: walk(run, b, ORDERS[run].names))


def kernel(**inputs):
    import numpy as _np
    import concourse.bacc as _bacc
    from concourse import mybir as _mybir
    from concourse.bass_utils import run_bass_kernel_spmd as _run

    a = {k: _np.asarray(v) for k, v in inputs.items()}

    def chunks(w):
        return w.reshape(w.shape[0] // P, P, w.shape[1]).transpose(1, 0, 2)

    pair = _np.concatenate([_np.arange(0, DK, 2), _np.arange(1, DK, 2)])
    rows = (_np.arange(H)[:, None] * DK + pair[None, :]).reshape(-1)
    wqk = _np.concatenate([a["L0_attn_Wq"][rows], a["L0_attn_Wk"][rows]], axis=0).T
    w2 = _np.concatenate([a["L0_ffn_W2"].reshape(MID, D), a["L0_ffn_b2"]], axis=0)

    rates = _np.float32(THETA) ** (-(_np.float32(2.0) * _np.arange(DK // 2, dtype=_np.float32)) / _np.float32(DK))
    angle = _np.arange(S, dtype=_np.float32)[:, None] * rates[None, :].astype(_np.float32)
    cos, sin = _np.cos(angle), _np.sin(angle)
    cos_t = _np.concatenate([cos, cos], axis=1).astype(_np.float32)
    sin_t = _np.concatenate([-sin, sin], axis=1).astype(_np.float32)

    spread = _np.concatenate([_np.repeat(_np.eye(PATHS), DM, axis=1), _np.eye(PATHS)], axis=1)

    sent = {
        "x": a["L0_attn_x"],
        "wqk": chunks(wqk),
        "wv": chunks(a["L0_attn_Wv"].T),
        "wo": chunks(a["L0_attn_Wo"].T),
        "mixk": chunks(a["L0_ffn_mix_kernel"].T),
        "w1": chunks(_np.concatenate([a["L0_ffn_W1"].transpose(1, 0, 2).reshape(D, MID),
                                      a["L0_ffn_Wo1"]], axis=1)),
        "b1": a["L0_ffn_b1"].reshape(MID)[:P * (NJ - 1)].reshape(NJ - 1, P).T,
        "b1_last": a["L0_ffn_b1"][PATHS - 1].reshape(DM, 1),
        "w2": w2,
        "bo1": a["L0_ffn_bo1"].reshape(DM, 1),
        "wo2": a["L0_ffn_Wo2"],
        "bo2": a["L0_ffn_bo2"],
        "gamma": a["L0_ffn_gamma"],
        "beta": a["L0_ffn_beta"],
        "cos_t": chunks(cos_t),
        "sin_t": chunks(sin_t),
        "ident": _np.eye(P, dtype=_np.float32),
        "spread": spread.astype(_np.float32),
        "order": _np.tile(_np.arange(PATHS, 0, -1, dtype=_np.float32), (P, 1)),
    }
    nc = _bacc.Bacc("TRN2", target_bir_lowering=False, num_devices=1)
    arrays, args = {}, {}
    for name, v in sent.items():
        v = _np.ascontiguousarray(v)
        arrays[f"in_{name}"] = v
        args[name] = nc.dram_tensor(f"in_{name}", v.shape, _mybir.dt.from_np(v.dtype), kind="ExternalInput").ap()
    args["out"] = nc.dram_tensor("out_0", (B, S, D), F32, kind="ExternalOutput").ap()
    build(nc, **args)
    r = _run(nc, [arrays], core_ids=[0])
    return r.results[0]["out_0"]
```
